# Optimizing a Trainium2 kernel written in Bass

```python
import numpy as np
import jax
import jax.numpy as jnp

def _softmax(x, axis=-1):
    return jax.nn.softmax(x, axis=axis)

def _gelu(x):
    return jax.nn.gelu(x, approximate=True)

def _silu(x):
    return jax.nn.silu(x)

def _sigmoid(x):
    return jax.nn.sigmoid(x)

def _layernorm(x, axis=-1, eps=1e-05):
    m = jnp.mean(x, axis=axis, keepdims=True)
    v = jnp.var(x, axis=axis, keepdims=True)
    return (x - m) / jnp.sqrt(v + eps)

def _scatter_add(tgt, idx, src, axis=0):
    return tgt.at[idx].add(src)

def _segment_sum(src, seg, n):
    return jax.ops.segment_sum(src, seg, n)
kernel_name = 'mk_flamingo_gated_d1_seqx_r4_226f30'

def setup_inputs(seed: int=0):
    np.random.seed(seed)
    _w = jnp.asarray

    def _rec_inputs():
        import jax
        import jax.numpy as jnp
        _rk = jax.random.key(seed)
        x = -0.0002928 + 1 * jax.random.normal(jax.random.fold_in(_rk, 1), (4, 512, 256), jnp.float32)
        _lenS = 512 - jax.random.randint(jax.random.fold_in(_rk, 7), (4,), 0, max(1, 512 // 4) + 1, jnp.int32)
        _lenS2 = 512 - jax.random.randint(jax.random.fold_in(_rk, 8), (4,), 0, max(1, 512 // 4) + 1, jnp.int32)
        _ctx_1024P = jax.random.normal(jax.random.fold_in(_rk, 11), (4, 16, 256), jnp.float32)
        _ctx_1024c = jax.random.dirichlet(jax.random.fold_in(_rk, 511), 0.3 * jnp.ones((16,), jnp.float32), (4, 512))
        _ctx_1024t = jnp.einsum('bsk,bkd->bsd', _ctx_1024c, _ctx_1024P)
        _ctx_1024t = _ctx_1024t * jax.lax.rsqrt(jnp.mean(jnp.square(_ctx_1024t)) + 1e-12) * 0.953939
        ctx_1024 = -1.39393e-06 + 0.999914 * (_ctx_1024t + 0.3 * jax.random.normal(jax.random.fold_in(_rk, 611), (4, 512, 256), jnp.float32))
        fside_BxSx3_0 = -0.00590116 + 1.0009 * jax.random.normal(jax.random.fold_in(_rk, 12), (4, 512, 3), jnp.float32)
        _g = jax.random.normal(jax.random.fold_in(_rk, 9001), (2, 1), jnp.float32)
        _g = jnp.sign(_g) * jnp.maximum(jnp.abs(_g), 1.0) + (_g == 0) * 1.0
        g_xattn = _g[0]
        g_ffn = _g[1]
        return (x, ctx_1024, fside_BxSx3_0, g_xattn, g_ffn)
    x, ctx_1024, fside_BxSx3_0, g_xattn, g_ffn = _rec_inputs()

    def _L0_xattn_setup():
        import jax, jax.numpy as jnp
        import numpy as np
        D_MODEL = 256
        NHEAD = 16
        HEAD_DIM = D_MODEL // NHEAD
        MAX_DIST = 5.0
        DIST_BINS = 32
        SCALE = float(np.sqrt(HEAD_DIM))
        key = jax.random.key(seed)
        ks = jax.random.split(key, 13)
        B, L = (2, 512)
        s = 1.0 / np.sqrt(D_MODEL)
        return {'query': jax.random.normal(ks[0], (B, L, D_MODEL), jnp.float32), 'key': jax.random.normal(ks[1], (B, L, D_MODEL), jnp.float32), 'value': jax.random.normal(ks[2], (B, L, D_MODEL), jnp.float32), 'positions': jax.random.normal(ks[3], (B, L, 3), jnp.float32), 'Wq': jax.random.normal(ks[4], (D_MODEL, D_MODEL), jnp.float32) * s, 'bq': jnp.zeros((D_MODEL,), jnp.float32), 'Wk': jax.random.normal(ks[5], (D_MODEL, D_MODEL), jnp.float32) * s, 'bk': jnp.zeros((D_MODEL,), jnp.float32), 'Wv': jax.random.normal(ks[6], (D_MODEL, D_MODEL), jnp.float32) * s, 'bv': jnp.zeros((D_MODEL,), jnp.float32), 'Wo': jax.random.normal(ks[7], (D_MODEL, D_MODEL), jnp.float32) * s, 'bo': jnp.zeros((D_MODEL,), jnp.float32), 'dist_emb': jax.random.normal(ks[8], (DIST_BINS + 1, NHEAD), jnp.float32) * 0.02}
    _L0_xattn_all = _L0_xattn_setup()
    _L0_xattn_in = {k: v for k, v in _L0_xattn_all.items() if k in ('Wq', 'bq', 'Wk', 'bk', 'Wv', 'bv', 'Wo', 'bo', 'dist_emb')}
    del _L0_xattn_all

    def _L0_ffn_setup():
        import jax, jax.numpy as jnp
        import numpy as np
        N_EXPERTS = 16
        TOP_K = 4
        HIDDEN = 256
        INTER = 128
        B, S = (2, 256)
        key = jax.random.key(seed)
        k1, k2, k3, k4, k5 = jax.random.split(key, 5)
        return {'hidden_states': jax.random.normal(k1, (B, S, HIDDEN), dtype=jnp.float32), 'gate_w': jax.random.normal(k2, (N_EXPERTS, HIDDEN), dtype=jnp.float32) * 0.02, 'w1': jax.random.normal(k3, (N_EXPERTS, HIDDEN, INTER), dtype=jnp.float32) * 0.02, 'w3': jax.random.normal(k4, (N_EXPERTS, HIDDEN, INTER), dtype=jnp.float32) * 0.02, 'w2': jax.random.normal(k5, (N_EXPERTS, INTER, HIDDEN), dtype=jnp.float32) * 0.02}
    _L0_ffn_all = _L0_ffn_setup()
    _L0_ffn_in = {k: v for k, v in _L0_ffn_all.items() if k in ('gate_w', 'w1', 'w3', 'w2')}
    del _L0_ffn_all
    return {'x': x, 'ctx_1024': ctx_1024, 'fside_BxSx3_0': fside_BxSx3_0, 'g_xattn': g_xattn, 'g_ffn': g_ffn, 'L0_xattn_Wq': _L0_xattn_in['Wq'], 'L0_xattn_bq': _L0_xattn_in['bq'], 'L0_xattn_Wk': _L0_xattn_in['Wk'], 'L0_xattn_bk': _L0_xattn_in['bk'], 'L0_xattn_Wv': _L0_xattn_in['Wv'], 'L0_xattn_bv': _L0_xattn_in['bv'], 'L0_xattn_Wo': _L0_xattn_in['Wo'], 'L0_xattn_bo': _L0_xattn_in['bo'], 'L0_xattn_dist_emb': _L0_xattn_in['dist_emb'], 'L0_ffn_gate_w': _L0_ffn_in['gate_w'], 'L0_ffn_w1': _L0_ffn_in['w1'], 'L0_ffn_w3': _L0_ffn_in['w3'], 'L0_ffn_w2': _L0_ffn_in['w2']}

def reference(x, ctx_1024, fside_BxSx3_0, g_xattn, g_ffn, L0_xattn_Wq, L0_xattn_bq, L0_xattn_Wk, L0_xattn_bk, L0_xattn_Wv, L0_xattn_bv, L0_xattn_Wo, L0_xattn_bo, L0_xattn_dist_emb, L0_ffn_gate_w, L0_ffn_w1, L0_ffn_w3, L0_ffn_w2):
    import jax
    import jax.numpy as jnp

    def _L0_xattn_ref(query, key, value, positions, Wq, bq, Wk, bk, Wv, bv, Wo, bo, dist_emb):
        import jax, jax.numpy as jnp
        import numpy as np
        D_MODEL = 256
        NHEAD = 16
        HEAD_DIM = D_MODEL // NHEAD
        MAX_DIST = 5.0
        DIST_BINS = 32
        SCALE = float(np.sqrt(HEAD_DIM))
        B, L, D = query.shape
        H, hd = (NHEAD, HEAD_DIM)
        Q = (query @ Wq + bq).reshape(B, L, H, hd).transpose(0, 2, 1, 3)
        K = (key @ Wk + bk).reshape(B, L, H, hd).transpose(0, 2, 1, 3)
        V = (value @ Wv + bv).reshape(B, L, H, hd).transpose(0, 2, 1, 3)
        scores = jnp.einsum('bhqd,bhkd->bhqk', Q, K) / SCALE
        diff = positions[:, :, None, :] - positions[:, None, :, :]
        dist = jnp.sqrt(jnp.sum(diff * diff, axis=-1))
        bins = jnp.clip((dist / MAX_DIST * DIST_BINS).astype(jnp.int32), 0, DIST_BINS)
        bias = dist_emb[bins].transpose(0, 3, 1, 2)
        attn = jax.nn.softmax(scores + bias, axis=-1)
        out = jnp.einsum('bhqk,bhkd->bhqd', attn, V)
        out = out.transpose(0, 2, 1, 3).reshape(B, L, D)
        return out @ Wo + bo

    def _L0_ffn_ref(hidden_states, gate_w, w1, w3, w2):
        import jax, jax.numpy as jnp
        import numpy as np
        N_EXPERTS = 16
        TOP_K = 4
        HIDDEN = 256
        INTER = 128
        B, S = (2, 256)
        'DeepseekV3 MoE adapter forward: router -> sparse scores -> expert GLU MLP -> combine.'
        b, s, h = hidden_states.shape
        x = hidden_states.reshape(-1, h)
        logits = jnp.einsum('th,eh->te', x, gate_w)
        probs = jax.nn.softmax(logits, axis=-1)
        topk_w, topk_idx = jax.lax.top_k(probs, TOP_K)
        topk_w = topk_w / jnp.sum(topk_w, axis=-1, keepdims=True)
        one_hot = (topk_idx[..., None] == jnp.arange(N_EXPERTS)).astype(topk_w.dtype)
        scores = jnp.einsum('tk,tke->te', topk_w, one_hot)
        g = jnp.einsum('th,ehi->tei', x, w1)
        u = jnp.einsum('th,ehi->tei', x, w3)
        act = jax.nn.silu(g) * u
        expert_out = jnp.einsum('tei,eih->teh', act, w2)
        out = jnp.einsum('teh,te->th', expert_out, scores)
        return out.reshape(b, s, h)
    x = x + jnp.tanh(g_xattn[0]) * _L0_xattn_ref(_layernorm(x, axis=-1), ctx_1024, ctx_1024, fside_BxSx3_0, L0_xattn_Wq, L0_xattn_bq, L0_xattn_Wk, L0_xattn_bk, L0_xattn_Wv, L0_xattn_bv, L0_xattn_Wo, L0_xattn_bo, L0_xattn_dist_emb)
    x = x + jnp.tanh(g_ffn[0]) * _L0_ffn_ref(_layernorm(x, axis=-1), L0_ffn_gate_w, L0_ffn_w1, L0_ffn_w3, L0_ffn_w2)
    return x

_drawn_inputs = setup_inputs


def setup_inputs(seed=0):
    import zlib

    import numpy as np

    out = dict(_drawn_inputs(seed))
    spreads = {'L0_xattn_bq': (0.0, 0.481),
     'L0_xattn_bk': (0.0, 2.0),
     'L0_xattn_bv': (0.0, 0.1),
     'L0_xattn_bo': (0.0, 0.1)}
    factors = {'fside_BxSx3_0': 200.0,
     'L0_xattn_dist_emb': 200.0,
     'L0_ffn_gate_w': 8.0,
     'L0_ffn_w1': 8.0,
     'L0_ffn_w3': 8.0,
     'L0_ffn_w2': 8.0}
    for name, (base, spread) in spreads.items():
        noise = np.random.default_rng([zlib.crc32(name.encode()), seed]).standard_normal(out[name].shape)
        drawn = base * np.exp(spread * noise) if base else spread * noise
        out[name] = jnp.asarray(drawn.astype(out[name].dtype))
    for name, factor in factors.items():
        out[name] = (out[name] * factor).astype(out[name].dtype)
    return out
```

```python
from contextlib import ExitStack

import numpy as np

import concourse.bass as bass
from concourse import mybir

ALU = mybir.AluOpType
ACT = mybir.ActivationFunctionType
F32 = mybir.dt.float32
BF16 = mybir.dt.bfloat16
F16 = mybir.dt.float16
I32 = mybir.dt.int32
AX = mybir.AxisListType
RMAX = bass.bass_isa.ReduceOp.max

P = 128
B, S, D = 4, 512, 256
H, HD = 16, 16
NT = S // P
C = D // P
G = 4
NG = H // G
STEPS = B * NG
BINS = 32
FAR = 1e30
E, TOPK, INTER = 16, 4, 128
PARTS = 3
QPART = [0, 0, 1, 0, 2, 1]
KPART = [0, 1, 0, 2, 0, 1]
NPROD = len(QPART)
ROWS = NPROD * HD
KROWS = ROWS + PARTS
EPS = 1e-5
XS, WS = 64.0, 16.0
QSCALE = 1.0 / float(np.sqrt(HD))
NP_RING = 8
NE = G * NT
NM = 8


def step_units():
    order = []
    for i in range(NM // 2):
        order += [("e", 3 * i), ("e", 3 * i + 1), ("m", 2 * i), ("e", 3 * i + 2), ("m", 2 * i + 1)]
    return order + [("t", 0)] + [("e", e) for e in range(3 * NM // 2, NE)]


def extras(s):
    b, g = divmod(s, NG)
    if s == -1:
        return [("xT", 0), ("q", 0), ("k", 0)]
    out = []
    if g == 0:
        out.append(("v", b))
        if b >= 2:
            out.append(("sc", b - 2))
    if g == 1:
        if b + 1 < B:
            out.append(("xT", b + 1))
        if b >= 1:
            out.append(("wo", b - 1))
    if g == 2:
        if b >= 1:
            out.append(("nT", b - 1))
        if b + 1 < B:
            out += [("q", b + 1), ("k", b + 1)]
    if g == 3 and b >= 1:
        out.append(("lg", b - 1))
    return out


LATE = {0: [("sc", B - 2), ("wo", B - 1)], 2: [("nT", B - 1)], 3: [("lg", B - 1)], 6: [("sc", B - 1)]}


def ring_order():
    order = list(extras(-1)) + [("m", 0)] * NM + [("t", 0)]
    for s in range(STEPS):
        order += extras(s)
        if s + 1 < STEPS:
            order += [("m", s + 1)] * NM + [("t", s + 1)]
    for n in range(B * E):
        order += [("gu", n)] + LATE.get(n, [])
    return order


RING = {what: n for n, what in enumerate(ring_order())}


def bin_thresholds():
    def binned(d2):
        return np.float32(np.sqrt(d2)) / np.float32(5.0) * np.float32(BINS)
    out = np.zeros((1, BINS + 1), np.float32)
    for j in range(1, BINS + 1):
        t = np.float32((5.0 * j / BINS) ** 2)
        while binned(np.nextafter(t, np.float32(0))) >= j:
            t = np.nextafter(t, np.float32(0))
        while binned(t) < j:
            t = np.nextafter(t, np.float32(np.inf))
        out[0, j] = t
    return out


THRESHOLDS = bin_thresholds()
NEAR = float(THRESHOLDS[0, BINS])


def gated_block(nc, x, ctx_t, pos, pos_cols, g_x, g_f, wq, wk, bqk_cols, wv, bv, wo, bo, emb, gate_t,
                w1, w3, w2, thr, out_t):
    q_dram = nc.dram_tensor("q_parts", (C, PARTS, P, S), BF16, kind="Internal").ap()
    k_dram = nc.dram_tensor("k_parts", (C, PARTS, P, S), BF16, kind="Internal").ap()
    sc_dram = nc.dram_tensor("scores", (E, B * S), F32, kind="Internal").ap()

    with ExitStack() as ctx:
        def sb(name, shape, dt=F32):
            return ctx.enter_context(nc.sbuf_tensor(name, shape, dt))

        def sem(name):
            return ctx.enter_context(nc.semaphore(name))

        W = [ctx.enter_context(nc.psum_tensor(f"W{i}", [P, 1024], F32)) for i in range(2)]
        SC = [ctx.enter_context(nc.psum_tensor(f"SC{i}", [P, S], F32)) for i in range(3)]
        O = ctx.enter_context(nc.psum_tensor("O", [P, S], F32))
        Y = [[SC[0], SC[1]], [SC[2], O]]

        ident = sb("ident", [P, P])
        ident_h = sb("ident_h", [P, P], F16)
        ident_w = sb("ident_w", [P, P])
        x_sb = sb("x_sb", [P, B * NT, D])
        xn = sb("xn", [P, NT, D])
        xnT = sb("xnT", [P, C, S])
        cT = sb("cT", [P, C, S])
        x2T = sb("x2T", [P, 2, C, B * S], F16)
        wq_sb, wk_sb, wv_sb = (sb(n, [P, C, D]) for n in ("wq_sb", "wk_sb", "wv_sb"))
        wo_sb = sb("wo_sb", [P, NG, D])
        bqk = sb("bqk", [P, 2, C])
        bv_sb = sb("bv_sb", [P, D])
        bo_sb = sb("bo_sb", [P, D])
        tg = sb("tg", [P, 2])
        etab = sb("etab", [P, BINS + 1, H])
        dtab = sb("dtab", [P, (BINS + 1) * H])
        gtab = sb("gtab", [P, (BINS + 1) * H])
        thr_sb = sb("thr_sb", [P, BINS + 1])
        diag = sb("diag", [P, 2, H, P], F16)
        qk32 = sb("qk32", [P, 2, S])
        parts = sb("parts", [P, 2, PARTS, S], BF16)
        Qst = sb("Qst", [P, H, S], BF16)
        Kst = sb("Kst", [P, H, S], BF16)
        V = sb("V", [P, NT * H, 2 * HD])
        mneg = sb("mneg", [P, H, NT])
        mtmp = sb("mtmp", [H, P])
        mpart = sb("mpart", [H, NG, PARTS, P], BF16)
        pr = sb("pr", [P, NP_RING, S])
        rec = sb("rec", [P, S])
        oT = sb("oT", [P, NG, S])
        pos_sb = sb("pos_sb", [P, S * 3])
        npos = sb("npos", [P, B * NT, 3])
        sq = sb("sq", [P, 3, S])
        d2 = sb("d2", [P, 2, NT, S])
        near = rec
        ext = sb("ext", [P, 2, 32])
        extr = sb("extr", [P, 2, 32])
        cmp_ = sb("cmp", [P, BINS])
        flags = sb("flags", [P, 2, 32], I32)
        st = sb("st", [P, NT, 6])
        mv = sb("mv", [P, NT, 2])
        veps = sb("veps", [P, NT])
        nhalf = sb("nhalf", [P, NT])
        rstd = sb("rstd", [P, NT])
        btmp = sb("btmp", [P, P])
        gate_sb = sb("gate_sb", [P, C, E])
        gate_h = sb("gate_h", [P, 2, C, E], F16)
        lg = sb("lg", [P, NT, E])
        pe = sb("pe", [P, NT, E + TOPK])
        top = sb("top", [P, NT, 8])
        mr = sb("mr", [P, NT, E + TOPK])
        r4 = sb("r4", [P, NT])
        score = sb("score", [P, NT, E])
        scT = sb("scT", [E, S])
        raw = sb("raw", [P, 2, 3 * D])
        w13a = sb("w13a", [P, 8 * 4 * 2 * P], F16)
        w13b = d2[:, :, :, :].rearrange("p a t s -> p (a t s)").bitcast(F16)
        w2s = pr[:, :, :].rearrange("p n s -> p (n s)").bitcast(F16).rearrange(
            "p (e l n) -> p e l n", e=E, l=2)

        def w13(e):
            t = w13a[:, :] if e < 8 else w13b
            return t.rearrange("p (e l m i) -> p e l m i", e=8, l=2, m=4)[:, e % 8]

        over_q = Qst[:, :, :].rearrange("p h s -> p (h s)").bitcast(F32)
        sg, t1, ac = (over_q[:, i * 2 * S:(i + 1) * 2 * S].rearrange("p (n s) -> p n s", n=2) for i in range(3))
        over_k = Kst[:, :, :].rearrange("p h s -> p (h s)").bitcast(F32)
        sbc = over_k[:, 0:3 * S].rearrange("p (n s) -> p n s", n=3)
        ahl = over_k[:, 3 * S:6 * S].bitcast(F16).rearrange("p (n l s) -> p n l s", n=3, l=2)
        osb = qk32


        in_x = [sem(f"in_x{b}") for b in range(B)]
        stack_in = [sem(f"stack_in{c}") for c in range(C)]
        in_ctx, in_pos, in_qkw, in_bqk, in_vow = (sem(n) for n in "in_ctx in_pos in_qkw in_bqk in_vow".split())
        in_small, in_gates, in_tab = (sem(n) for n in "in_small in_gates in_tab".split())
        in_raw = [sem(f"in_raw{i}") for i in range(2)]
        in_scores = [sem(f"in_scores{i}") for i in range(3)]
        w_full, w_free = sem("w_full"), sem("w_free")
        idents, wo_zero, ones_set, tabs_done, tg_done, npos_done = (
            sem(n) for n in "idents wo_zero ones_set tabs_done tg_done npos_done".split())
        veps_done, rstd_done, xn_done, yn_done, xb_done = (
            sem(n) for n in "veps_done rstd_done xn_done yn_done xb_done".split())
        qk_full, parts_done, v_done = (
            sem(n) for n in "qk_full parts_done v_done".split())
        parts_out = [sem(f"parts_out{i}") for i in range(2)]
        sq_done, d2_sum, d2_done, ext_done, extr_done, step_done = (
            sem(n) for n in "sq_done d2_sum d2_done ext_done extr_done step_done".split())
        m_done, m_split, m_in, qk_done, granted, exp_done, pv_done = (
            sem(n) for n in "m_done m_split m_in qk_done granted exp_done pv_done".split())
        oT_done, lg_done, lgexp_done, score_done, scT_done, sc_out = (
            sem(n) for n in "oT_done lg_done lgexp_done score_done scT_done sc_out".split())
        whi_done, wlo_done, silu_done, t1_done, act_done, w2_used = (
            sem(n) for n in "whi_done wlo_done silu_done t1_done act_done w2_used".split())
        near_tiles = sem("near_tiles")
        osb_done, out_done = sem("osb_done"), sem("out_done")
        dve_chain, pool_chain = sem("dve_chain"), sem("pool_chain")

        block = ctx.enter_context(nc.Block())
        EXPS = STEPS * NE

        def row(ap):
            return ap.rearrange("(o n) -> o n", o=1).broadcast_to([P, ap.shape[0]])

        @block.sync
        def _(sp):
            def load_x(b):
                sp.dma_start(x_sb[:, b * NT:(b + 1) * NT, :],
                             x[b].rearrange("(t p) d -> p t d", p=P)).then_inc(in_x[b], 16)

            def load_ctx(b):
                if b:
                    sp.wait_ge(w_full, RING["v", b - 1] + 1)
                sp.dma_start(cT[:, :, :], ctx_t[:, b * S:(b + 1) * S].rearrange("(c p) s -> p c s", p=P)
                             ).then_inc(in_ctx, 16)

            def load_pos(b):
                if b:
                    sp.wait_ge(sq_done, NT * b)
                sp.dma_start(pos_sb[:, :], pos[b:b + 1, :].broadcast_to([P, S * 3])).then_inc(in_pos, 16)

            def store_parts(b):
                if b:
                    sp.wait_ge(stack_in[1], 192 * b)
                for i in range(2 * C):
                    n = 2 * C * b + i
                    sp.wait_ge(parts_done, n + 1)
                    sp.dma_start((k_dram if i >= C else q_dram)[i % C].rearrange("a p s -> p a s"),
                                 parts[:, n % 2, :, :]).then_inc(parts_out[n % 2], 16)

            def load_stacks(b, c):
                for out in parts_out:
                    sp.wait_ge(out, 16 * C * (b + 1))
                if b:
                    sp.wait_ge(qk_done, NE * ((b - 1) * NG + 2 * c + 2))
                for stack, dram, order in ((Qst, q_dram, QPART), (Kst, k_dram, KPART)):
                    for g in range(NPROD):
                        sp.dma_start(stack[g * HD:(g + 1) * HD, 8 * c:8 * c + 8, :],
                                     dram[c, order[g]].rearrange("(h d) s -> d h s", d=HD)
                                     ).then_inc(stack_in[c], 16)

            def load_max_rows(s):
                g = s % NG
                sp.wait_ge(m_split, s + 1)
                for i in range(PARTS):
                    sp.dma_start(Qst[ROWS + i:ROWS + i + 1, G * g:G * g + G, :].rearrange(
                        "o h (t q) -> o (h t) q", q=P), mpart[:, g, i, :]).then_inc(m_in, 16)

            def store_scores(b):
                sp.wait_ge(scT_done, b + 1)
                sp.dma_start(sc_dram[:, b * S:(b + 1) * S], scT[:, :]).then_inc(sc_out, 16)

            load_x(0)
            load_ctx(0)
            for w, t in ((wq, wq_sb), (wk, wk_sb)):
                sp.dma_start(t[:, :, :], w.rearrange("(c p) n -> p c n", p=P)).then_inc(in_qkw, 16)
            load_pos(0)
            for b in range(1, B):
                load_x(b)
            store_parts(0)
            load_stacks(0, 0)
            load_stacks(0, 1)
            for s in range(-1, STEPS):
                b, g = divmod(s, NG)
                if s >= 0 and b + 1 < B:
                    if g == 0:
                        load_pos(b + 1)
                    if g == 1:
                        load_ctx(b + 1)
                    if g == 2:
                        store_parts(b + 1)
                        load_stacks(b + 1, 0)
                if g == 0 and b >= 1:
                    load_stacks(b, 1)
                if s + 1 < STEPS:
                    load_max_rows(s + 1)
                if g == 0 and b >= 2:
                    store_scores(b - 2)

            def load_expert(e):
                if e >= 2:
                    sp.wait_ge(wlo_done, e - 1)
                r = raw[:, e % 2, :]
                for i, w in enumerate((w1, w3)):
                    sp.dma_start(r[:, i * D:(i + 1) * D].rearrange("p (c i) -> p c i", c=C),
                                 w[e].rearrange("(c p) i -> p c i", p=P)).then_inc(in_raw[e % 2], 16)
                sp.dma_start(r[:, 2 * D:3 * D], w2[e]).then_inc(in_raw[e % 2], 16)

            def load_scores(n):
                b, e = divmod(n, E)
                if n == 0:
                    sp.wait_ge(qk_done, EXPS)
                if e == 0:
                    sp.wait_ge(sc_out, 16 * (b + 1))
                if n >= 3:
                    sp.wait_ge(t1_done, n - 2)
                sp.dma_start(sbc[:, n % 3, :], sc_dram[e:e + 1, b * S:(b + 1) * S].broadcast_to([P, S])
                             ).then_inc(in_scores[n % 3], 16)

            def store_out(b):
                sp.wait_ge(osb_done, b + 1)
                sp.dma_start(out_t[:, b * S:(b + 1) * S].rearrange("(c p) s -> p c s", p=P),
                             osb[:, :, :]).then_inc(out_done, 16)

            load_expert(0)
            load_expert(1)
            for n in range(B * E):
                if n + 2 < E:
                    load_expert(n + 2)
                load_scores(n)
                if n == 5:
                    store_scores(B - 2)
                if n == 9:
                    store_scores(B - 1)
                if n % E == 8 and n >= E:
                    store_out(n // E - 1)
            store_out(B - 1)
            sp.wait_ge(out_done, 16 * B)

        @block.gpsimd
        def _(pool):
            links = [0]

            def link(ins):
                links[0] += 1
                ins.then_inc(pool_chain, 1)
                pool.wait_ge(pool_chain, links[0])

            pool.memset(nhalf[:, :], -0.5)
            link(pool.memset(ident[:, :], 0.0))
            link(pool.affine_select(out=ident[:, :], in_=ident[:, :], compare_op=ALU.not_equal, fill=1.0,
                                    base=0, pattern=[[-1, P]], channel_multiplier=1))
            pool.tensor_copy(ident_h[:, :], ident[:, :])
            pool.tensor_scalar(ident_w[:, :], ident[:, :], WS, None, ALU.mult).then_inc(idents, 1)
            pool.memset(wo_sb[:, :, :], 0.0).then_inc(wo_zero, 1)
            pool.memset(pe[:, :, E:E + TOPK], -1.0)
            pool.memset(ext[:, :, :], 0.0)
            pool.memset(V[:, :, HD:2 * HD], 1.0).then_inc(ones_set, 1)
            powers = [0]

            def power():
                powers[0] += 1
                pool.wait_ge(veps_done, powers[0])
                pool.tensor_tensor(rstd[:, :], veps[:, :], nhalf[:, :], ALU.pow).then_inc(rstd_done, 1)

            def split(n):
                pool.wait_ge(qk_full, n + 1)
                if n >= 2:
                    pool.wait_ge(parts_out[n % 2], 16 * (n // 2))
                h, m, l = (parts[:, n % 2, k, :] for k in range(PARTS))
                v = qk32[:, n % 2, :]
                link(pool.tensor_copy(h, v))
                link(pool.tensor_tensor(v, v, h, ALU.subtract))
                link(pool.tensor_copy(m, v))
                pool.tensor_tensor(l, v, m, ALU.subtract).then_inc(parts_done, 1)

            def distances(b):
                if b >= 2:
                    pool.wait_ge(step_done, (b - 1) * NG)
                for r in range(NT):
                    n = b * NT + r
                    pool.wait_ge(sq_done, n + 1)
                    o = d2[:, b % 2, r, :]
                    link(pool.tensor_tensor(o, sq[:, 0, :], sq[:, 1, :], ALU.add))
                    pool.tensor_tensor(o, o, sq[:, 2, :], ALU.add).then_inc(d2_sum, 1)
                    pool.wait_ge(d2_sum, n + 1)
                    own = o[:, r * P:(r + 1) * P]
                    pool.affine_select(out=own, in_=own, compare_op=ALU.not_equal, fill=FAR, base=0,
                                       pattern=[[-1, P]], channel_multiplier=1).then_inc(d2_done, 1)

            def reduce_extremes(b):
                pool.wait_ge(ext_done, b + 1)
                pool.partition_all_reduce(extr[:, b % 2, :], ext[:, b % 2, :], P, RMAX).then_inc(extr_done, 1)

            def residual(b):
                pool.wait_ge(xn_done, b + 1)
                if b == 0:
                    pool.wait_ge(tabs_done, 1)
                xs = x_sb[:, b * NT:(b + 1) * NT, :]
                pool.tensor_tensor(xs, xs, bo_sb[:, None, :].broadcast_to([P, NT, D]), ALU.add).then_inc(xb_done, 1)

            power()
            for n in range(2 * C):
                split(n)
            distances(0)
            reduce_extremes(0)
            residual(0)
            for s in range(STEPS):
                b, g = divmod(s, NG)
                if g == 0 and b + 1 < B:
                    power()
                    residual(b + 1)
                if g == 1:
                    if b + 1 < B:
                        distances(b + 1)
                    if b >= 1:
                        power()
                if g == 2 and b + 1 < B:
                    for n in range(2 * C * (b + 1), 2 * C * (b + 2)):
                        split(n)
                    reduce_extremes(b + 1)
            for n in range(B * E):
                if n == 1:
                    power()
                pool.wait_ge(silu_done, n + 1)
                pool.wait_ge(in_scores[n % 3], 16 * (n // 3 + 1))
                if n >= 2:
                    pool.wait_ge(act_done, n - 1)
                pool.tensor_tensor(t1[:, n % 2, :], sg[:, n % 2, :], sbc[:, n % 3, :], ALU.mult).then_inc(t1_done, 1)

        @block.scalar
        def _(act):
            act.dma_start(npos[:, :, :], pos_cols).then_inc(in_small, 16)
            act.dma_start(bqk[:, :, :], bqk_cols).then_inc(in_bqk, 16)
            act.dma_start(tg[:, 0:1], row(g_x)).then_inc(in_gates, 16)
            act.dma_start(tg[:, 1:2], row(g_f)).then_inc(in_gates, 16)
            act.dma_start(etab[:, :, :].rearrange("p j h -> p (j h)"),
                          emb.rearrange("(o j) h -> o (j h)", o=1).broadcast_to([P, (BINS + 1) * H])).then_inc(in_tab, 16)
            act.dma_start(thr_sb[:, :], thr.broadcast_to([P, BINS + 1])).then_inc(in_tab, 16)
            act.dma_start(gate_sb[:, :, :], gate_t.rearrange("(c p) e -> p c e", p=P)).then_inc(in_tab, 16)
            act.dma_start(bo_sb[:, :], row(bo)).then_inc(in_tab, 16)
            act.dma_start(wv_sb[:, :, :], wv.rearrange("(c p) n -> p c n", p=P)).then_inc(in_vow, 16)
            act.dma_start(bv_sb[:, :], row(bv)).then_inc(in_vow, 16)
            act.wait_ge(wo_zero, 1)
            for j in range(G):
                act.dma_start(wo_sb[32 * j:32 * j + HD, :, :],
                              wo.rearrange("(g j d) n -> j d g n", g=NG, j=G)[j]).then_inc(in_vow, 16)
            act.wait_ge(in_gates, 32)
            nc.scalar.activation(tg[:, :], tg[:, :], ACT.Tanh).then_inc(tg_done, 1)
            act.wait_ge(in_small, 16)
            nc.scalar.mul(npos[:, :, :], npos[:, :, :], -1.0).then_inc(npos_done, 1)
            act.wait_ge(npos_done, 1)

            def squares(n):
                act.wait_ge(in_pos, 16 * (n // NT + 1))
                if n:
                    act.wait_ge(d2_sum, n)
                v = pos_sb[:, :].rearrange("p (s a) -> p a s", a=3)
                for a in range(3):
                    ins = nc.scalar.activation(sq[:, a, :], v[:, a, :], ACT.Square, bias=npos[:, n, a:a + 1])
                ins.then_inc(sq_done, 1)

            def router_exp(b):
                act.wait_ge(lg_done, b + 1)
                nc.scalar.activation(pe[:, :, 0:E], lg[:, :, :], ACT.Exp, scale=1.0 / (XS * WS)).then_inc(lgexp_done, 1)

            for n in range(NT):
                squares(n)
            for s in range(STEPS):
                b, g = divmod(s, NG)
                for e in range(NE):
                    n = s * NE + e
                    act.wait_ge(qk_done, n + 1)
                    act.wait_ge(granted, n + 1)
                    if n >= NP_RING:
                        act.wait_ge(pv_done, (n - NP_RING) // G + 1)
                    nc.scalar.activation(pr[:, n % NP_RING, :], SC[n % 3][:, :], ACT.Exp).then_inc(exp_done, 1)
                    if g == 1 and b + 1 < B and e % 4 == 2:
                        squares((b + 1) * NT + e // 4)
                    if g == 3 and b >= 1 and e == 6:
                        router_exp(b - 1)

            def split_high(e):
                act.wait_ge(in_raw[e % 2], 48 * (e // 2 + 1))
                if e == 0:
                    act.wait_ge(pv_done, STEPS * NT)
                if e == 8:
                    act.wait_ge(step_done, STEPS)
                nc.scalar.activation(w13(e)[:, 0, :, :], raw[:, e % 2, 0:2 * D].rearrange("p (m i) -> p m i", i=P),
                                     ACT.Copy, scale=WS)
                nc.scalar.activation(w2s[:, e, 0, :], raw[:, e % 2, 2 * D:3 * D], ACT.Copy, scale=WS).then_inc(whi_done, 1)

            split_high(0)
            split_high(1)
            for n in range(B * E):
                w = RING["gu", n]
                act.wait_ge(w_full, w + 1)
                if n >= 2:
                    act.wait_ge(t1_done, n - 1)
                nc.scalar.activation(sg[:, n % 2, :], W[w % 2][:, 0:S], ACT.Silu, scale=1.0 / (XS * WS)).then_inc(silu_done, 1)
                if n + 2 < E:
                    split_high(n + 2)
                if n == 4:
                    router_exp(B - 1)

        @block.vector
        def _(dve):
            links, w, norms = [0], [0], [0]

            def link(ins):
                links[0] += 1
                ins.then_inc(dve_chain, 1)
                dve.wait_ge(dve_chain, links[0])

            def slot():
                dve.wait_ge(w_full, w[0] + 1)
                return W[w[0] % 2]

            def used(ins):
                w[0] += 1
                ins.then_inc(w_free, 1)

            def norm_stats(b):
                for t in range(NT):
                    ins = dve.bn_stats(st[:, t, :], x_sb[:, b * NT + t, :])
                link(ins)
                for t in range(NT):
                    ins = dve.bn_aggr(mv[:, t, :], st[:, t, :])
                link(ins)
                dve.tensor_scalar(veps[:, :], mv[:, :, 1], EPS, None, ALU.add).then_inc(veps_done, 1)

            def normalise(b, scale, done):
                norms[0] += 1
                dve.wait_ge(rstd_done, norms[0])
                if scale != 1.0:
                    link(dve.tensor_scalar(rstd[:, :], rstd[:, :], scale, None, ALU.mult))
                for t in range(NT):
                    ins = dve.tensor_scalar(xn[:, t, :], x_sb[:, b * NT + t, :], mv[:, t, 0:1], rstd[:, t:t + 1],
                                            ALU.subtract, ALU.mult)
                ins.then_inc(done, 1)

            def extremes(b):
                dve.wait_ge(d2_done, NT * (b + 1))
                if b >= 2:
                    dve.wait_ge(extr_done, b - 1)
                d, x_ = d2[:, b % 2, :, :], ext[:, b % 2, :]
                dve.tensor_reduce(x_[:, 0:16], d.rearrange("p r (c q) -> p (r c) q", q=P), AX.X, ALU.min, negate=True)
                for r in range(NT):
                    link(dve.scalar_tensor_tensor(out=near[:, :], in0=d[:, r, :], scalar=NEAR, in1=d[:, r, :],
                                                  op0=ALU.is_lt, op1=ALU.mult))
                    link(dve.tensor_reduce(x_[:, 16 + r:17 + r], near[:, :], AX.X, ALU.max))
                dve.tensor_reduce(x_[:, 20:21], x_[:, 0:16], AX.X, ALU.max)
                dve.tensor_reduce(x_[:, 21:22], x_[:, 16:20], AX.X, ALU.max).then_inc(ext_done, 1)

            regs = {}

            def near_flags(b):
                dve.wait_ge(extr_done, b + 1)
                x_, f = extr[:, b % 2, :], flags[:, b % 2, :]
                link(dve.tensor_scalar(f[:, 0:21], x_[:, 0:21], -NEAR, None, ALU.is_gt))
                link(dve.tensor_scalar(x_[:, 20:21], x_[:, 20:21], -1.0, None, ALU.mult))
                for i in range(2):
                    link(dve.tensor_scalar(cmp_[:, :], thr_sb[:, 1:BINS + 1], x_[:, 20 + i:21 + i], None, ALU.is_le))
                    link(dve.tensor_reduce(x_[:, 24 + i:25 + i], cmp_[:, :], AX.X, ALU.add))
                link(dve.tensor_copy(f[:, 21:23], x_[:, 24:26]))
                regs[b] = [dve.value_load(flags[0:1, b % 2, i:i + 1], min_val=0, max_val=BINS) for i in (20, 21, 22)]

            def correct(tile, b, r, h):
                _, lo, hi = regs[b]
                with dve.Fori(0, NT) as c:
                    f = dve.value_load(flags[0:1, b % 2, bass.ds(r * NT + c, 1)], min_val=0, max_val=1)
                    with dve.If(f > 0):
                        dist = d2[:, b % 2, bass.ds(r, 1), bass.ds(c * P, P)].rearrange("p a q -> p (a q)")
                        part = tile[:, bass.ds(c * P, P)]
                        dve.tensor_scalar(btmp[:, :], dist, NEAR, dtab[:, bass.ds(hi * H + h, 1)], ALU.is_lt, ALU.mult)
                        dve.drain()
                        dve.tensor_tensor(part, part, btmp[:, :], ALU.add)
                        dve.drain()
                        with dve.If(hi > lo):
                            with dve.Fori(lo + 1, hi + 1) as j:
                                dve.tensor_scalar(btmp[:, :], dist, thr_sb[:, bass.ds(j, 1)],
                                                  gtab[:, bass.ds(j * H + h, 1)], ALU.is_lt, ALU.mult)
                                dve.drain()
                                dve.tensor_tensor(part, part, btmp[:, :], ALU.add)
                                dve.drain()

            def row_max(s, qt, pair, tile):
                h = G * (s % NG) + 2 * pair
                out = mneg[:, h:h + 2, bass.ds(qt, 1)].rearrange("p h o -> p (h o)")
                return dve.tensor_reduce(out, tile[:, :].rearrange("p (h k) -> p h k", h=2), AX.X, ALU.max, negate=True)

            def exp_tile(s, e, bank):
                b, g = divmod(s, NG)
                dve.wait_ge(qk_done, e + (s * NE + 1))
                dve.sem_inc(near_tiles, 1)
                correct(SC[bank], b, e // G, e % G + G * g)
                dve.drain().then_inc(granted, 1)

            def max_slot(s, i, k, base):
                b, g = divmod(s, NG)
                dve.wait_ge(w_full, i * 2 + (base + k + 1))
                dve.sem_inc(near_tiles, 1)
                t = W[(base + k) % 2]
                for h in range(2):
                    correct(t[:, h * S:(h + 1) * S], b, i, G * g + 2 * k + h)
                row_max(s, i, k, t)
                dve.drain().then_inc(w_free, 1)

            def units(s):
                b, nb = max(s, 0) // NG, min(s + 1, STEPS - 1) // NG
                base = w[0]
                with dve.If(regs[b][0] + regs[nb][0] > 0):
                    with dve.Fori(0, NM // 2) as i:
                        for k in range(2):
                            if s >= 0:
                                for j in ((0, 1), (2,))[k]:
                                    exp_tile(s, i * 3 + j, (s * NE + j) % 3)
                            if s + 1 < STEPS:
                                max_slot(s + 1, i, k, base)
                with dve.Else():
                    if s >= 0:
                        dve.sem_inc(granted, NE)
                    for m in range(NM if s + 1 < STEPS else 0):
                        dve.wait_ge(w_full, base + m + 1)
                        row_max(s + 1, m // 2, m % 2, W[(base + m) % 2]).then_inc(w_free, 1)
                if s + 1 < STEPS:
                    w[0] = base + NM
                    dve.drain().then_inc(m_done, 1)
                    max_parts(s + 1)
                if s >= 0:
                    with dve.If(regs[b][0] > 0):
                        for e in range(3 * NM // 2, NE):
                            exp_tile(s, e, (s * NE + e) % 3)
                    with dve.If(regs[b][0] < 1):
                        with dve.If(regs[nb][0] > 0):
                            dve.sem_inc(granted, NE - 3 * NM // 2)
                dve.drain().then_inc(step_done, 1)

            def max_parts(s):
                g = s % NG
                t = slot()[0:H, 0:P]
                link(dve.tensor_copy(mpart[:, g, 0, :], t))
                for i in range(1, PARTS):
                    link(dve.tensor_tensor(mtmp[:, :], t if i == 1 else mtmp[:, :], mpart[:, g, i - 1, :], ALU.subtract))
                    if i + 1 < PARTS:
                        link(dve.tensor_copy(mpart[:, g, i, :], mtmp[:, :]))
                dve.tensor_copy(mpart[:, g, PARTS - 1, :], mtmp[:, :]).then_inc(m_split, 1)
                w[0] += 1
                dve.drain().then_inc(w_free, 1)

            def norm_out(s):
                dve.wait_ge(pv_done, NT * (s + 1))
                link(dve.stream_shuffle(rec[:, :], O[:, :], list(range(HD, 2 * HD)) * 2))
                link(dve.reciprocal(rec[:, :], rec[:, :]))
                dve.tensor_tensor(oT[:, s % NG, :], O[:, :], rec[:, :], ALU.mult).then_inc(oT_done, 1)
                dve.wait_ge(oT_done, s + 1)

            def router(b):
                def per_token(v):
                    return v[:, :, None].broadcast_to([P, NT, E])

                dve.wait_ge(lgexp_done, b + 1)
                p_ = pe[:, :, 0:E]
                link(dve.tensor_reduce(r4[:, :], p_, AX.X, ALU.add))
                link(dve.reciprocal(r4[:, :], r4[:, :]))
                link(dve.tensor_tensor(p_, p_, per_token(r4), ALU.mult))
                for t in range(NT):
                    ins = dve.max(top[:, t, :], pe[:, t, 0:E])
                link(ins)
                link(dve.memset(top[:, :, TOPK:8], -1.0))
                for t in range(NT):
                    ins = dve.match_replace(mr[:, t, :], top[:, t, :], pe[:, t, :], -2.0)
                link(ins)
                link(dve.scalar_tensor_tensor(out=score[:, :, :], in0=mr[:, :, 0:E], scalar=-1.5, in1=p_,
                                              op0=ALU.is_lt, op1=ALU.mult))
                link(dve.tensor_reduce(r4[:, :], score[:, :, :], AX.X, ALU.add))
                link(dve.reciprocal(r4[:, :], r4[:, :]))
                link(dve.tensor_scalar(r4[:, :], r4[:, :], tg[:, 1:2], None, ALU.mult))
                dve.tensor_tensor(score[:, :, :], score[:, :, :], per_token(r4), ALU.mult).then_inc(score_done, 1)

            def extra(kind, b):
                if kind == "sc":
                    router(b)
                    if b:
                        dve.wait_ge(sc_out, 16 * b)
                t = slot()
                if kind == "xT":
                    used(dve.tensor_copy(xnT[:, :, :].rearrange("p c s -> p (c s)"), t[:, :]))
                elif kind == "q" or kind == "k":
                    i = "qk".index(kind)
                    for c in range(C):
                        n = 2 * C * b + C * i + c
                        if n >= 2:
                            dve.wait_ge(parts_done, n - 1)
                        ins = dve.tensor_scalar(qk32[:, n % 2, :], t[:, c * S:(c + 1) * S], bqk[:, i, c:c + 1],
                                                (QSCALE, 1.0)[i], ALU.add, ALU.mult).then_inc(qk_full, 1)
                    w[0] += 1
                    dve.drain().then_inc(w_free, 1)
                elif kind == "v":
                    dve.wait_ge(pv_done, NT * NG * b) if b else dve.wait_ge(ones_set, 1)
                    used(dve.tensor_tensor(V[:, :, 0:HD].rearrange("p (t h) d -> p t h d", t=NT),
                                           t[:, :].rearrange("p (t h d) -> p t h d", t=NT, h=H),
                                           bv_sb[:, :].rearrange("p (o h d) -> p o h d", o=1, h=H).broadcast_to([P, NT, H, HD]),
                                           ALU.add))
                elif kind == "wo":
                    dve.wait_ge(xb_done, b + 1)
                    xs = x_sb[:, b * NT:(b + 1) * NT, :].rearrange("p t d -> p (t d)")
                    used(dve.scalar_tensor_tensor(out=xs, in0=t[:, :], scalar=tg[:, 0:1], in1=xs,
                                                  op0=ALU.mult, op1=ALU.add))
                    dve.wait_ge(w_free, w[0])
                    norm_stats(b)
                elif kind == "nT":
                    cols = slice(b * S, (b + 1) * S)
                    t3 = t[:, :].rearrange("p (c s) -> p c s", c=C)
                    link(dve.tensor_copy(x2T[:, 0, :, cols], t3))
                    used(dve.tensor_tensor(x2T[:, 1, :, cols], t3, x2T[:, 0, :, cols], ALU.subtract))
                elif kind == "lg":
                    t3 = t[:, 0:NT * E].rearrange("p (t e) -> p t e", t=NT)
                    link(dve.tensor_reduce(r4[:, :], t3, AX.X, ALU.max))
                    dve.tensor_tensor(lg[:, :, :], t3, r4[:, :, None].broadcast_to([P, NT, E]),
                                      ALU.subtract).then_inc(lg_done, 1)
                    w[0] += 1
                    dve.drain().then_inc(w_free, 1)
                elif kind == "sc":
                    dve.tensor_copy(scT[:, :], t[0:E, 0:S]).then_inc(scT_done, 1)
                    w[0] += 1
                    dve.drain().then_inc(w_free, 1)

            dve.memset(Kst[ROWS:KROWS, :, :], 1.0)
            dve.wait_ge(in_x[0], 16)
            norm_stats(0)
            dve.wait_ge(in_tab, 64)
            dve.wait_ge(tg_done, 1)
            dve.wait_ge(idents, 1)
            dve.memset(top[:, :, :], -1.0)
            link(dve.tensor_tensor(dtab[:, :].rearrange("p (j h) -> p j h", h=H), etab[:, :, :],
                                   etab[:, BINS:BINS + 1, :].broadcast_to([P, BINS + 1, H]), ALU.subtract))
            dve.tensor_tensor(gtab[:, H:], etab[:, 0:BINS, :].rearrange("p j h -> p (j h)"),
                              etab[:, 1:BINS + 1, :].rearrange("p j h -> p (j h)"), ALU.subtract)
            dve.tensor_scalar(bo_sb[:, :], bo_sb[:, :], tg[:, 0:1], None, ALU.mult).then_inc(tabs_done, 1)
            normalise(0, 1.0, xn_done)
            for h in range(H):
                ins = dve.tensor_scalar(diag[:, 0, h, :], ident[:, :], dtab[:, h:h + 1], None, ALU.mult)
            link(ins)
            for h in range(H):
                dve.scalar_tensor_tensor(out=diag[:, 1, h, :], in0=ident[:, :], scalar=dtab[:, h:h + 1],
                                         in1=diag[:, 0, h, :], op0=ALU.mult, op1=ALU.subtract)
            link(dve.tensor_scalar(gate_h[:, 0, :, :], gate_sb[:, :, :], WS, None, ALU.mult))
            dve.scalar_tensor_tensor(out=gate_h[:, 1, :, :], in0=gate_sb[:, :, :], scalar=WS, in1=gate_h[:, 0, :, :],
                                     op0=ALU.mult, op1=ALU.subtract).then_inc(tabs_done, 1)
            dve.wait_ge(in_bqk, 16)
            for kind, b in extras(-1):
                extra(kind, b)
            extremes(0)
            near_flags(0)
            units(-1)
            dve.wait_ge(in_vow, 16 * 6)
            for s in range(STEPS):
                b, g = divmod(s, NG)
                for kind, eb in extras(s):
                    extra(kind, eb)
                if s >= 1:
                    norm_out(s - 1)
                if b + 1 < B:
                    if g == 0:
                        dve.wait_ge(in_x[b + 1], 16)
                        norm_stats(b + 1)
                    if g == 2:
                        extremes(b + 1)
                    if g == 3:
                        near_flags(b + 1)
                units(s)
                if g == 0 and b + 1 < B:
                    normalise(b + 1, 1.0, xn_done)
                if g == 1 and b >= 1:
                    normalise(b - 1, XS, yn_done)

            def split_low(e):
                dve.wait_ge(whi_done, e + 1)
                r = raw[:, e % 2, :]
                dve.scalar_tensor_tensor(out=w13(e)[:, 1, :, :].rearrange("p m i -> p (m i)"), in0=r[:, 0:2 * D], scalar=WS,
                                         in1=w13(e)[:, 0, :, :].rearrange("p m i -> p (m i)"), op0=ALU.mult, op1=ALU.subtract)
                dve.scalar_tensor_tensor(out=w2s[:, e, 1, :], in0=r[:, 2 * D:3 * D], scalar=WS, in1=w2s[:, e, 0, :],
                                         op0=ALU.mult, op1=ALU.subtract).then_inc(wlo_done, 1)

            def result(b):
                dve.wait_ge(w2_used, E * (b + 1))
                if b:
                    dve.wait_ge(out_done, 16 * b)
                for c in range(C):
                    ins = dve.tensor_scalar(osb[:, c, :], Y[b % 2][c][:, :], 1.0 / WS, None, ALU.mult)
                ins.then_inc(osb_done, 1)

            split_low(0)
            split_low(1)
            norm_out(STEPS - 1)
            for n in range(B * E):
                t = slot()
                dve.wait_ge(t1_done, n + 1)
                used(dve.scalar_tensor_tensor(out=ac[:, n % 2, :], in0=t[:, S:2 * S], scalar=1.0 / (XS * WS),
                                              in1=t1[:, n % 2, :], op0=ALU.mult, op1=ALU.mult))
                dve.wait_ge(w_free, w[0])
                if n >= 3:
                    dve.wait_ge(w2_used, n - 2)
                link(dve.tensor_copy(ahl[:, n % 3, 0, :], ac[:, n % 2, :]))
                dve.tensor_tensor(ahl[:, n % 3, 1, :], ac[:, n % 2, :], ahl[:, n % 3, 0, :], ALU.subtract).then_inc(act_done, 1)
                if n + 2 < E:
                    split_low(n + 2)
                for kind, b in LATE.get(n, []):
                    extra(kind, b)
                if n == 1:
                    normalise(B - 1, XS, yn_done)
                if n % E == 2 and n >= E:
                    result(n // E - 1)
            result(B - 1)

        @block.tensor
        def _(pe_):
            mm, w, o_n = nc.tensor.matmul, [0], [0]

            def slot():
                if w[0] >= 2:
                    pe_.wait_ge(w_free, w[0] - 1)
                return W[w[0] % 2]

            def full(ins):
                w[0] += 1
                ins.then_inc(w_full, 1)

            def transposes(t):
                for c in range(C):
                    for k in range(NT):
                        ins = nc.tensor.transpose(t[:, c * S + k * P:c * S + (k + 1) * P], xn[:, k, c * P:(c + 1) * P],
                                                  ident[:, :])
                full(ins)

            def extra(kind, b):
                if kind == "xT":
                    pe_.wait_ge(xn_done, b + 1)
                elif kind == "q":
                    pe_.wait_ge(w_free, RING["xT", b] + 1)
                    if b == 0:
                        pe_.wait_ge(in_qkw, 32)
                elif kind == "k":
                    pe_.wait_ge(in_ctx, 16 * (b + 1))
                elif kind == "v" and b == 0:
                    pe_.wait_ge(in_vow, 16 * 6)
                elif kind == "wo":
                    pe_.wait_ge(oT_done, NG * (b + 1))
                elif kind == "nT":
                    pe_.wait_ge(yn_done, b + 1)
                elif kind == "lg":
                    pe_.wait_ge(w_free, RING["nT", b] + 1)
                    pe_.wait_ge(tabs_done, 2)
                elif kind == "sc":
                    pe_.wait_ge(score_done, b + 1)
                t = slot()
                if kind == "xT" or kind == "nT":
                    transposes(t)
                elif kind == "q" or kind == "k":
                    wt, src = (wq_sb, xnT) if kind == "q" else (wk_sb, cT)
                    for c in range(C):
                        for k in range(C):
                            ins = mm(t[:, c * S:(c + 1) * S], wt[:, k, c * P:(c + 1) * P], src[:, k, :],
                                     start=(k == 0), stop=(k == C - 1))
                    full(ins)
                elif kind == "v":
                    for k in range(NT):
                        for c in range(C):
                            ins = mm(t[:, k * D:(k + 1) * D], cT[:, c, k * P:(k + 1) * P], wv_sb[:, c, :],
                                     start=(c == 0), stop=(c == C - 1))
                    full(ins)
                elif kind == "wo":
                    for k in range(NT):
                        for g in range(NG):
                            ins = mm(t[:, k * D:(k + 1) * D], oT[:, g, k * P:(k + 1) * P], wo_sb[:, g, :],
                                     start=(g == 0), stop=(g == NG - 1))
                    full(ins)
                elif kind == "lg":
                    pairs = [(c, i, j) for c in range(C) for i, j in ((0, 0), (0, 1), (1, 0))]
                    for k in range(NT):
                        for m, (c, i, j) in enumerate(pairs):
                            ins = mm(t[:, k * E:(k + 1) * E], x2T[:, i, c, b * S + k * P:b * S + (k + 1) * P],
                                     gate_h[:, j, c, :], start=(m == 0), stop=(m == len(pairs) - 1))
                    full(ins)
                elif kind == "sc":
                    for k in range(NT):
                        ins = nc.tensor.transpose(t[0:E, k * P:(k + 1) * P], score[:, k, :], ident[:, :])
                    full(ins)

            def exp_scores(s, e):
                b, g = divmod(s, NG)
                n, r, h = s * NE + e, e // G, G * g + e % G
                if e == 0:
                    pe_.wait_ge(m_in, 16 * PARTS * (s + 1))
                if n >= 3:
                    pe_.wait_ge(exp_done, n - 2)
                mm(SC[n % 3][:, :], Kst[0:KROWS, h, r * P:(r + 1) * P], Qst[0:KROWS, h, :], start=True, stop=False,
                   skip_group_check=True)
                for i in range(2):
                    ins = mm(SC[n % 3][:, r * P:(r + 1) * P], ident_h[:, :], diag[:, i, h, :], start=False,
                             stop=(i == 1), skip_group_check=True)
                ins.then_inc(qk_done, 1)

            def max_scores(s, m):
                b, g = divmod(s, NG)
                r = m // 2
                if m == 0 and g % 2 == 0:
                    pe_.wait_ge(stack_in[g // 2], 192 * (b + 1))
                t = slot()
                for i in range(2):
                    h = G * g + 2 * (m % 2) + i
                    mm(t[:, i * S:(i + 1) * S], Qst[0:ROWS, h, r * P:(r + 1) * P], Kst[0:ROWS, h, :],
                       start=True, stop=False, skip_group_check=True)
                    ins = mm(t[:, i * S + r * P:i * S + (r + 1) * P], ident_h[:, :], diag[:, 0, h, :],
                             start=False, stop=True, skip_group_check=True)
                full(ins)

            def max_transpose(s):
                pe_.wait_ge(m_done, s + 1)
                g = s % NG
                full(nc.tensor.transpose(slot()[0:H, 0:P], mneg[:, G * g:G * g + G, :].rearrange("p h t -> p (h t)"),
                                         ident[:, :]))

            def values(s, r):
                b, g = divmod(s, NG)
                if r == 0:
                    if s:
                        pe_.wait_ge(oT_done, s)
                    if g == 0:
                        pe_.wait_ge(w_free, RING["v", b] + 1)
                pe_.wait_ge(exp_done, s * NE + (r + 1) * G)
                for j in range(G):
                    n = s * NE + r * G + j
                    ins = mm(O[32 * j:32 * j + 32, :], V[:, r * H + G * g + j, :], pr[:, n % NP_RING, :],
                             start=(r == 0), stop=(r == NT - 1), skip_group_check=True)
                ins.then_inc(pv_done, 1)

            pe_.wait_ge(idents, 1)
            for kind, b in extras(-1):
                extra(kind, b)
            pe_.wait_ge(tabs_done, 2)
            pe_.wait_ge(ones_set, 1)
            for s in range(-1, STEPS):
                late = s >= 1
                if s >= 0:
                    for kind, b in extras(s):
                        extra(kind, b)
                        if late:
                            values(s - 1, NT - 1)
                            late = False
                for kind, i in step_units():
                    if kind == "e" and s >= 0:
                        exp_scores(s, i)
                        if i == 1 and late:
                            values(s - 1, NT - 1)
                        if i % G == 1 and i > G:
                            values(s, i // G - 1)
                    if kind == "m" and s + 1 < STEPS:
                        max_scores(s + 1, i)
                    if kind == "t" and s + 1 < STEPS:
                        max_transpose(s + 1)

            def gate_up(n):
                b, e = divmod(n, E)
                if b == 0:
                    pe_.wait_ge(wlo_done, e + 1)
                if e == 0:
                    pe_.wait_ge(w_free, RING["nT", b] + 1)
                t = slot()
                for m in range(2):
                    pairs = [(c, i, j) for c in range(C) for i, j in ((0, 0), (0, 1), (1, 0))]
                    for k, (c, i, j) in enumerate(pairs):
                        ins = mm(t[:, m * S:(m + 1) * S], w13(e)[:, i, C * m + c, :], x2T[:, j, c, b * S:(b + 1) * S],
                                 start=(k == 0), stop=(k == len(pairs) - 1))
                full(ins)

            def down(n):
                b, e = divmod(n, E)
                pe_.wait_ge(act_done, n + 1)
                if n == 0:
                    pe_.wait_ge(exp_done, EXPS)
                if n == E:
                    pe_.wait_ge(oT_done, STEPS)
                if e == 0 and b >= 2:
                    pe_.wait_ge(osb_done, b - 1)
                y = Y[b % 2]
                for c in range(C):
                    for k, (i, j) in enumerate(((0, 0), (0, 1), (1, 0))):
                        ins = mm(y[c][:, :], w2s[:, e, i, c * P:(c + 1) * P], ahl[:, n % 3, j, :],
                                 start=(e == 0 and k == 0), stop=(e == E - 1 and k == 2), skip_group_check=True)
                ins.then_inc(w2_used, 1)
                if e == 0:
                    for c in range(C):
                        for k in range(NT):
                            mm(y[c][:, k * P:(k + 1) * P], x_sb[:, b * NT + k, c * P:(c + 1) * P], ident_w[:, :],
                               start=False, stop=False, skip_group_check=True)

            values(STEPS - 1, NT - 1)
            for n in range(B * E):
                gate_up(n)
                for kind, b in LATE.get(n, []):
                    extra(kind, b)
                if n >= 2:
                    down(n - 2)
            down(B * E - 2)
            down(B * E - 1)


def kernel(**inputs):
    import concourse.bacc as bacc
    from concourse.bass_utils import run_bass_kernel_spmd

    a = {k: np.asarray(v) for k, v in inputs.items()}
    pos_ = a["fside_BxSx3_0"]
    given = {
        "x": a["x"],
        "ctx_t": a["ctx_1024"].reshape(B * S, D).T,
        "pos": pos_.reshape(B, S * 3),
        "pos_cols": pos_.reshape(B * NT, P, 3).transpose(1, 0, 2),
        "g_x": a["g_xattn"], "g_f": a["g_ffn"],
        "wq": a["L0_xattn_Wq"], "wk": a["L0_xattn_Wk"],
        "bqk_cols": np.stack([a["L0_xattn_bq"].reshape(C, P), a["L0_xattn_bk"].reshape(C, P)]).transpose(2, 0, 1),
        "wv": a["L0_xattn_Wv"], "bv": a["L0_xattn_bv"], "wo": a["L0_xattn_Wo"], "bo": a["L0_xattn_bo"],
        "emb": a["L0_xattn_dist_emb"], "gate_t": a["L0_ffn_gate_w"].T,
        "w1": a["L0_ffn_w1"], "w3": a["L0_ffn_w3"], "w2": a["L0_ffn_w2"], "thr": THRESHOLDS,
    }
    nc = bacc.Bacc("TRN2", target_bir_lowering=False, num_devices=1)
    arrays, args = {}, {}
    for name, v in given.items():
        v = np.ascontiguousarray(v)
        arrays[f"in_{name}"] = v
        args[name] = nc.dram_tensor(f"in_{name}", v.shape, mybir.dt.from_np(v.dtype), kind="ExternalInput").ap()
    args["out_t"] = nc.dram_tensor("out_t", (D, B * S), F32, kind="ExternalOutput").ap()
    gated_block(nc, **args)
    got = run_bass_kernel_spmd(nc, [arrays], core_ids=[0]).results[0]["out_t"]
    return np.ascontiguousarray(got.T).reshape(B, S, D)
```

```python
from contextlib import ExitStack

import numpy as np

import concourse.bass as bass
from concourse import mybir

ALU = mybir.AluOpType
ACT = mybir.ActivationFunctionType
F32 = mybir.dt.float32
BF16 = mybir.dt.bfloat16
F16 = mybir.dt.float16
I32 = mybir.dt.int32
AX = mybir.AxisListType
RMAX = bass.bass_isa.ReduceOp.max

P = 128
B, S, D = 4, 512, 256
H, HD = 16, 16
NT = S // P
C = D // P
G = 4
NG = H // G
STEPS = B * NG
BINS = 32
FAR = 1e30
E, TOPK, INTER = 16, 4, 128
PARTS = 3
QPART = [0, 0, 1, 0, 2, 1]
KPART = [0, 1, 0, 2, 0, 1]
NPROD = len(QPART)
ROWS = NPROD * HD
NSLOT = 8
NROWS = ROWS + PARTS * NSLOT
KROWS = NROWS + PARTS
STACK_DMAS = 2 * NPROD + PARTS + 1
EPS = 1e-5
XS, WS = 64.0, 16.0
QSCALE = 1.0 / float(np.sqrt(HD))
NP_RING = 8
NE = G * NT
NM = 8


def step_units(s, half):
    order = [("t", s + 1)] if half and s + 1 < STEPS else []
    for i in range(half * NM // 2, (half + 1) * NM // 2):
        order.append(("x", i))
        slots = [(s + 1, NM // 2 + i)] if half == 0 else [(s + 2, i - NM // 2)]
        if s == -1 and half == 0:
            slots = [(0, 2 * i), (0, 2 * i + 1)]
        order += [("m", m) for m in slots if m[0] < STEPS]
        if s >= 0:
            order += [("e", 2 * i), ("e", 2 * i + 1)]
    return order


def extras(s, place):
    b, g = divmod(s, NG)
    if s == -1:
        return {0: [("k", 0), ("xT", 0), ("q", 0), ("rk", 0), ("nr", 0)]}.get(place, [])
    prev, nxt = b >= 1, b + 1 < B
    return [(kind, c) for where, at, kind, c, there in (
        (0, 0, "v", b, True), (0, 2, "k", b + 1, nxt), (0, 4, "wo", b - 1, prev),
        (1, 0, "xT", b + 1, nxt), (1, 2, "q", b + 1, nxt), (1, 3, "rk", b + 1, nxt), (1, 4, "nr", b + 1, nxt),
        (2, 3, "nT", b - 1, prev), (2, 6, "lg", b - 1, prev), (3, 5, "sc", b - 1, prev),
    ) if (where, at) == (g, place) and there]


BY_ACT = ("k", "xT", "q")

LATE = {2: [("wo", B - 1)], 10: [("nT", B - 1)], 12: [("lg", B - 1)], 17: [("sc", B - 1)]}


def ring_order():
    order = []
    for s in range(-1, STEPS):
        for half in range(2):
            for kind, i in step_units(s, half):
                order += extras(s, i) if kind == "x" else [(kind, i)] if kind in "mt" else []
    for n in range(B * E):
        order += [("gu", n)] + LATE.get(n, [])
    return order


RING = {what: n for n, what in enumerate(ring_order())}


def norm_order():
    order = [("x", 0), ("x", 1)]
    for b in range(B):
        order += [("y", b - 1)] * (b >= 1) + [("x", b + 2)] * (b + 2 < B)
    return order + [("y", B - 1)]


NORM = {what: n for n, what in enumerate(norm_order())}


def bin_thresholds():
    def binned(d2):
        return np.float32(np.sqrt(d2)) / np.float32(5.0) * np.float32(BINS)
    out = np.zeros((1, BINS + 1), np.float32)
    for j in range(1, BINS + 1):
        t = np.float32((5.0 * j / BINS) ** 2)
        while binned(np.nextafter(t, np.float32(0))) >= j:
            t = np.nextafter(t, np.float32(0))
        while binned(t) < j:
            t = np.nextafter(t, np.float32(np.inf))
        out[0, j] = t
    return out


TWO_ONES = float(np.array([0x3F803F80], np.uint32).view(np.float32)[0])
THRESHOLDS = bin_thresholds()
NEAR = float(THRESHOLDS[0, BINS])


def gated_block(nc, x, ctx_t, pos, pos_cols, g_x, g_f, wq, wk, bqk_cols, wv, bv, wo, bo, emb, emb_rows, gate_t,
                w1, w3, w2, nthr, slots, out_t):
    q_dram = nc.dram_tensor("q_parts", (C, PARTS, P, S), BF16, kind="Internal").ap()
    k_dram = nc.dram_tensor("k_parts", (C, PARTS, P, S), BF16, kind="Internal").ap()
    nq_dram = nc.dram_tensor("near_bias", (PARTS, P, S), BF16, kind="Internal").ap()
    nk_dram = nc.dram_tensor("near_keys", (P, S), BF16, kind="Internal").ap()
    sc_dram = nc.dram_tensor("scores", (E, B * S), F32, kind="Internal").ap()

    with ExitStack() as ctx:
        def sb(name, shape, dt=F32):
            return ctx.enter_context(nc.sbuf_tensor(name, shape, dt))

        def sem(name):
            return ctx.enter_context(nc.semaphore(name))

        W = [ctx.enter_context(nc.psum_tensor(f"W{i}", [P, 1024], F32)) for i in range(2)]
        SC = [ctx.enter_context(nc.psum_tensor(f"SC{i}", [P, S], F32)) for i in range(3)]
        O = ctx.enter_context(nc.psum_tensor("O", [P, S], F32))
        Y = [[SC[0], SC[1]], [SC[2], O]]

        ident = sb("ident", [P, P])
        ident_h = sb("ident_h", [P, P], F16)
        ident_w = sb("ident_w", [P, P])
        x_sb = sb("x_sb", [P, B * NT, D])
        xn = sb("xn", [P, NT, D])
        xnT = sb("xnT", [P, C, S])
        cT = sb("cT", [P, C, S])
        x2T = sb("x2T", [P, 2, C, B * S], F16)
        wq_sb, wk_sb, wv_sb = (sb(n, [P, C, D]) for n in ("wq_sb", "wk_sb", "wv_sb"))
        wo_sb = sb("wo_sb", [P, NG, D])
        bqk = sb("bqk", [P, 2, C])
        bv_sb = sb("bv_sb", [P, D])
        bo_sb = sb("bo_sb", [P, D])
        tg = sb("tg", [P, 2])
        dtab = sb("dtab", [P, (BINS + 1) * H])
        gtab = sb("gtab", [P, (BINS + 1) * H])
        erow = sb("erow", [P, BINS + 1])
        drow = sb("drow", [P, BINS + 1])
        grow = sb("grow", [P, BINS + 1])
        nthr_sb = sb("nthr_sb", [P, BINS + 1])
        slot_of = sb("slot_of", [P, P])
        before = sb("before", [P, P])
        ones = sb("ones", [P, P])
        diag = sb("diag", [P, 2, H, P], F16)
        qk32 = sb("qk32", [P, 2, S])
        parts = sb("parts", [P, 2, PARTS, S], BF16)
        Qst = sb("Qst", [P, H, S], BF16)
        Kst = sb("Kst", [P, H, S], BF16)
        V = sb("V", [P, NT * H, 2 * HD])
        mneg = sb("mneg", [P, H, NT])
        mtmp = sb("mtmp", [H, P])
        mpart = sb("mpart", [H, NG, PARTS, P], BF16)
        pr = sb("pr", [P, NP_RING, S])
        rec = sb("rec", [P, S])
        rs = sb("rs", [P, S // 32])
        oT = sb("oT", [P, NG, S])
        pos_sb = sb("pos_sb", [P, S * 3])
        npos = sb("npos", [P, B * NT, 3])
        d2 = sb("d2", [P, 2, NT, S])
        m8 = sb("m8", [P, NT, 8])
        near8 = sb("near8", [P, NT, 8])
        nf = sb("nf", [P, NT + 1])
        nslot = sb("nslot", [P, NT])
        few = sb("few", [P, 2])
        ext = sb("ext", [P, 2])
        extr = sb("extr", [P, 2])
        cmp_ = sb("cmp", [P, BINS])
        flags_f = sb("flags_f", [P, 4])
        flags = sb("flags", [P, B, 4], I32)
        st = sb("st", [P, NT, 6])
        mv = sb("mv", [P, NT, 2])
        veps = sb("veps", [P, NT])
        nhalf = sb("nhalf", [P, NT])
        rstd = sb("rstd", [P, NT])
        gate_sb = sb("gate_sb", [P, C, E])
        gate_h = sb("gate_h", [P, 2, C, E], F16)
        lg = sb("lg", [P, NT, E])
        pe = sb("pe", [P, NT, E + TOPK])
        top = sb("top", [P, NT, 8])
        mr = sb("mr", [P, NT, E + TOPK])
        r4 = sb("r4", [P, NT])
        score = sb("score", [P, NT, E])
        scT = sb("scT", [E, S])
        sq = sb("sq", [P, 2, 3, S])
        w13a = sb("w13a", [P, 8 * 4 * 2 * P], F16)
        early = w13a[:, :].bitcast(F32)
        sel, brow, btmp = (early[:, i * S:(i + 1) * S] for i in range(3))
        nparts = early[:, 3 * S:3 * S + PARTS * S // 2].bitcast(BF16).rearrange("p (a s) -> p a s", a=PARTS)
        etab = early[:, 6 * S:6 * S + (BINS + 1) * H].rearrange("p (j h) -> p j h", h=H)
        selT = early[:, 5 * S:5 * S + S // 2].bitcast(BF16)
        raw = sq[:, 0, :, :].rearrange("p a s -> p (a s)").rearrange("p (n m) -> p n m", n=2)
        w13b = d2[:, :, :, :].rearrange("p a t s -> p (a t s)").bitcast(F16)
        w2s = pr[:, :, :].rearrange("p n s -> p (n s)").bitcast(F16).rearrange(
            "p (e l n) -> p e l n", e=E, l=2)

        def w13(e):
            t = w13a[:, :] if e < 8 else w13b
            return t.rearrange("p (e l m i) -> p e l m i", e=8, l=2, m=4)[:, e % 8]

        over_q = Qst[:, :, :].rearrange("p h s -> p (h s)").bitcast(F32)
        sg, t1, ac = (over_q[:, i * 2 * S:(i + 1) * 2 * S].rearrange("p (n s) -> p n s", n=2) for i in range(3))
        over_k = Kst[:, :, :].rearrange("p h s -> p (h s)").bitcast(F32)
        sbc = over_k[:, 0:3 * S].rearrange("p (n s) -> p n s", n=3)
        ahl = over_k[:, 3 * S:6 * S].bitcast(F16).rearrange("p (n l s) -> p n l s", n=3, l=2)
        osb = qk32


        in_x = [sem(f"in_x{b}") for b in range(B)]
        stack_in = [sem(f"stack_in{c}") for c in range(C)]
        in_ctx, in_pos, in_qkw, in_bqk, in_vow = (sem(n) for n in "in_ctx in_pos in_qkw in_bqk in_vow".split())
        in_small, in_gates, in_tab = (sem(n) for n in "in_small in_gates in_tab".split())
        in_raw = [sem(f"in_raw{i}") for i in range(2)]
        in_scores = [sem(f"in_scores{i}") for i in range(3)]
        w_full, w_free = sem("w_full"), [sem(f"w_free{i}") for i in range(2)]
        idents, wo_zero, ones_set, tabs_done, tg_done, npos_done = (
            sem(n) for n in "idents wo_zero ones_set tabs_done tg_done npos_done".split())
        veps_done, rstd_done, norm_done, xb_done, x2h_done, bq_scaled = (
            sem(n) for n in "veps_done rstd_done norm_done xb_done x2h_done bq_scaled".split())
        qk_full, parts_done = (sem(n) for n in "qk_full parts_done".split())
        parts_out = [sem(f"parts_out{i}") for i in range(2)]
        sq_done, d2_sum, d2_done, ext_done, extr_done, step_done = (
            sem(n) for n in "sq_done d2_sum d2_done ext_done extr_done step_done".split())
        m_done, m_split, m_in, qk_done, granted, exp_done, pv_done = (
            sem(n) for n in "m_done m_split m_in qk_done granted exp_done pv_done".split())
        oT_done, lg_done, lgexp_done, score_done, scT_done, sc_out = (
            sem(n) for n in "oT_done lg_done lgexp_done score_done scT_done sc_out".split())
        w13_high, w13_low, w2_high, w2_low, silu_done, t1_done, act_done, w2_used = (
            sem(n) for n in "w13_high w13_low w2_high w2_low silu_done t1_done act_done w2_used".split())
        osb_done, out_done = sem("osb_done"), sem("out_done")
        nf_done, sel_done, rows_done, rows_out = (sem(n) for n in "nf_done sel_done rows_done rows_out".split())
        sq_neg = sem("sq_neg")
        dve_chain, pool_chain = sem("dve_chain"), sem("pool_chain")

        block = ctx.enter_context(nc.Block())
        EXPS = STEPS * NE

        def freed(n):
            return w_free[n % 2], n // 2 + 1

        def row(ap):
            return ap.rearrange("(o n) -> o n", o=1).broadcast_to([P, ap.shape[0]])

        @block.sync
        def _(sp):
            def load_x(b):
                sp.dma_start(x_sb[:, b * NT:(b + 1) * NT, :],
                             x[b].rearrange("(t p) d -> p t d", p=P)).then_inc(in_x[b], 16)

            def load_ctx(b):
                if b:
                    sp.wait_ge(w_full, RING["v", b - 1] + 1)
                sp.dma_start(cT[:, :, :], ctx_t[:, b * S:(b + 1) * S].rearrange("(c p) s -> p c s", p=P)
                             ).then_inc(in_ctx, 16)

            def load_pos(b):
                if b:
                    sp.wait_ge(sq_done, NT * b)
                sp.dma_start(pos_sb[:, :], pos[b:b + 1, :].broadcast_to([P, S * 3])).then_inc(in_pos, 16)

            def store_parts(b, which):
                if b:
                    sp.wait_ge(stack_in[1], 16 * STACK_DMAS * b)
                for i in which:
                    n = 2 * C * b + i
                    sp.wait_ge(parts_done, n + 1)
                    sp.dma_start((q_dram if i >= C else k_dram)[i % C].rearrange("a p s -> p a s"),
                                 parts[:, n % 2, :, :]).then_inc(parts_out[n % 2], 16)

            def store_rows(b):
                sp.wait_ge(rows_done, b + 1)
                sp.dma_start(nk_dram, selT).then_inc(rows_out, 16)
                sp.dma_start(nq_dram.rearrange("a p s -> p a s"), nparts).then_inc(rows_out, 16)

            def load_stacks(b, c):
                for out in parts_out:
                    sp.wait_ge(out, 16 * C * (b + 1))
                if b:
                    sp.wait_ge(qk_done, NE * ((b - 1) * NG + 2 * c + 2))
                for stack, dram, order in ((Kst, k_dram, KPART), (Qst, q_dram, QPART)):
                    for g in range(NPROD):
                        sp.dma_start(stack[g * HD:(g + 1) * HD, 8 * c:8 * c + 8, :],
                                     dram[c, order[g]].rearrange("(h d) s -> d h s", d=HD)
                                     ).then_inc(stack_in[c], 16)

            def load_rows(b, c):
                sp.wait_ge(rows_out, 32 * (b + 1))
                for i in range(PARTS):
                    sp.dma_start(Kst[ROWS + i * NSLOT:ROWS + (i + 1) * NSLOT, 8 * c:8 * c + 8, :],
                                 nk_dram.rearrange("(n h) s -> n h s", h=H)[:, 8 * c:8 * c + 8, :]
                                 ).then_inc(stack_in[c], 16)
                sp.dma_start(Qst[ROWS:NROWS, 8 * c:8 * c + 8, :],
                             nq_dram.rearrange("a (n h) s -> (a n) h s", h=H)[:, 8 * c:8 * c + 8, :]
                             ).then_inc(stack_in[c], 16)

            def load_max_rows(s):
                g = s % NG
                sp.wait_ge(m_split, s + 1)
                for i in range(PARTS):
                    sp.dma_start(Qst[NROWS + i:NROWS + i + 1, G * g:G * g + G, :].rearrange(
                        "o h (t q) -> o (h t) q", q=P), mpart[:, g, i, :]).then_inc(m_in, 16)

            def store_scores(b):
                sp.wait_ge(scT_done, b + 1)
                sp.dma_start(sc_dram[:, b * S:(b + 1) * S], scT[:, :]).then_inc(sc_out, 16)

            def load_expert(e):
                if e >= 2:
                    sp.wait_ge(w2_low, e - 1)
                if e == 0:
                    sp.wait_ge(d2_sum, NT * B)
                r = raw[:, e % 2, :]
                for i, w in enumerate((w1, w3)):
                    sp.dma_start(r[:, i * D:(i + 1) * D].rearrange("p (c i) -> p c i", c=C),
                                 w[e].rearrange("(c p) i -> p c i", p=P)).then_inc(in_raw[e % 2], 16)
                sp.dma_start(r[:, 2 * D:3 * D], w2[e]).then_inc(in_raw[e % 2], 16)

            load_ctx(0)
            load_x(0)
            for w, t in ((wk, wk_sb), (wq, wq_sb)):
                sp.dma_start(t[:, :, :], w.rearrange("(c p) n -> p c n", p=P)).then_inc(in_qkw, 16)
            load_pos(0)
            for b in range(1, B):
                load_x(b)
            store_parts(0, range(2 * C))
            load_stacks(0, 0)
            store_rows(0)
            load_rows(0, 0)
            load_stacks(0, 1)
            load_rows(0, 1)
            load_pos(1)
            load_max_rows(0)
            for s in range(STEPS):
                b, g = divmod(s, NG)
                more = b + 1 < B
                if g == 0:
                    if more:
                        load_ctx(b + 1)
                    if b:
                        load_stacks(b, 1)
                        load_rows(b, 1)
                if g == 1 and more:
                    store_parts(b + 1, range(C, 2 * C))
                    if b + 2 < B:
                        load_pos(b + 2)
                if g == 2 and more:
                    load_stacks(b + 1, 0)
                    load_rows(b + 1, 0)
                if s + 1 < STEPS:
                    load_max_rows(s + 1)
                if g == 0 and more:
                    store_parts(b + 1, range(C))
                if g == 1 and more:
                    store_rows(b + 1)
                if s == STEPS - 3:
                    load_expert(0)
                    load_expert(1)
                if g == 3 and b:
                    store_scores(b - 1)

            def load_scores(n):
                b, e = divmod(n, E)
                if n == 0:
                    sp.wait_ge(qk_done, EXPS)
                if e == 0:
                    sp.wait_ge(sc_out, 16 * (b + 1))
                if n >= 3:
                    sp.wait_ge(t1_done, n - 2)
                sp.dma_start(sbc[:, n % 3, :], sc_dram[e:e + 1, b * S:(b + 1) * S].broadcast_to([P, S])
                             ).then_inc(in_scores[n % 3], 16)

            def store_out(b):
                sp.wait_ge(osb_done, b + 1)
                sp.dma_start(out_t[:, b * S:(b + 1) * S].rearrange("(c p) s -> p c s", p=P),
                             osb[:, :, :]).then_inc(out_done, 16)

            for n in range(B * E):
                if n + 2 < E:
                    load_expert(n + 2)
                load_scores(n)
                if n == 19:
                    store_scores(B - 1)
                if n % E == 8 and n >= E:
                    store_out(n // E - 1)
            store_out(B - 1)
            sp.wait_ge(out_done, 16 * B)

        @block.gpsimd
        def _(pool):
            links = [0]

            def link(ins):
                links[0] += 1
                ins.then_inc(pool_chain, 1)
                pool.wait_ge(pool_chain, links[0])

            pool.memset(nhalf[:, :], -0.5)
            link(pool.memset(ident[:, :], 0.0))
            link(pool.affine_select(out=ident[:, :], in_=ident[:, :], compare_op=ALU.not_equal, fill=1.0,
                                    base=0, pattern=[[-1, P]], channel_multiplier=1))
            pool.tensor_copy(ident_h[:, :], ident[:, :])
            pool.tensor_scalar(ident_w[:, :], ident[:, :], WS, None, ALU.mult).then_inc(idents, 1)
            pool.memset(wo_sb[:, :, :], 0.0).then_inc(wo_zero, 1)
            pool.memset(pe[:, :, E:E + TOPK], -1.0)
            pool.memset(nf[:, NT:], 0.0)
            pool.memset(nparts, 0.0)
            link(pool.memset(ones[:, :], 1.0))
            pool.affine_select(out=before[:, :], in_=ones[:, :], compare_op=ALU.is_gt, fill=0.0,
                               base=0, pattern=[[1, P]], channel_multiplier=-1)
            pool.memset(V[:, :, HD:2 * HD], 1.0).then_inc(ones_set, 1)
            def norm_rstd(what, b):
                n = NORM[what, b]
                pool.wait_ge(veps_done, n + 1)
                if what == "y" and b + 2 < B:
                    pool.wait_ge(w_full, RING["xT", b + 2] + 1)
                elif what == "y":
                    pool.wait_ge(w_full, RING["nT", b - 1] + 1)
                elif b >= 3:
                    pool.wait_ge(w_full, RING["nT", b - 3] + 1)
                elif b:
                    pool.wait_ge(w_full, RING["xT", b - 1] + 1)
                link(pool.tensor_tensor(rstd[:, :], veps[:, :], nhalf[:, :], ALU.pow))
                if what == "y":
                    link(pool.tensor_scalar(rstd[:, :], rstd[:, :], XS, None, ALU.mult))

            def norm_tile(b, t):
                return pool.tensor_scalar(xn[:, t, :], x_sb[:, b * NT + t, :], mv[:, t, 0:1], rstd[:, t:t + 1],
                                          ALU.subtract, ALU.mult)

            def normalise(what, b):
                norm_rstd(what, b)
                for t in range(NT):
                    ins = norm_tile(b, t)
                ins.then_inc(norm_done, 1)
                pool.wait_ge(norm_done, NORM[what, b] + 1)

            def split(n):
                pool.wait_ge(qk_full, n + 1)
                if n >= 2:
                    pool.wait_ge(parts_out[n % 2], 16 * (n // 2))
                h, m, l = (parts[:, n % 2, k, :] for k in range(PARTS))
                v = qk32[:, n % 2, :]
                link(pool.tensor_scalar(h, v, 1.0, 1.0, ALU.mult, ALU.mult))
                link(pool.tensor_tensor(v, v, h, ALU.subtract))
                link(pool.tensor_scalar(m, v, 1.0, 1.0, ALU.mult, ALU.mult))
                pool.tensor_tensor(l, v, m, ALU.subtract).then_inc(parts_done, 1)

            def distances(b, tiles):
                if b >= 2:
                    pool.wait_ge(step_done, (b - 1) * NG)
                for r in tiles:
                    n = b * NT + r
                    pool.wait_ge(sq_done, n + 1)
                    o = d2[:, b % 2, r, :]
                    link(pool.tensor_tensor(o, sq[:, n % 2, 0, :], sq[:, n % 2, 1, :], ALU.add))
                    pool.tensor_tensor(o, sq[:, n % 2, 2, :], o, ALU.subtract).then_inc(d2_sum, 1)
                    pool.wait_ge(d2_sum, n + 1)
                    own = o[:, r * P:(r + 1) * P]
                    pool.affine_select(out=own, in_=own, compare_op=ALU.not_equal, fill=-FAR, base=0,
                                       pattern=[[-1, P]], channel_multiplier=1).then_inc(d2_done, 1)

            def reduce_extremes(b):
                pool.wait_ge(ext_done, b + 1)
                pool.partition_all_reduce(extr[:, :], ext[:, :], P, RMAX).then_inc(extr_done, 1)

            def residual(b):
                if b == 0:
                    pool.wait_ge(tabs_done, 1)
                xs = x_sb[:, b * NT:(b + 1) * NT, :]
                pool.tensor_tensor(xs, xs, bo_sb[:, None, :].broadcast_to([P, NT, D]), ALU.add).then_inc(xb_done, 1)

            norm_rstd("x", 0)
            pool.sem_inc(rstd_done, 1)
            distances(0, range(NT))
            reduce_extremes(0)
            residual(0)
            for s in range(STEPS):
                b, g = divmod(s, NG)
                if s == 0:
                    normalise("x", 1)
                if b + 1 < B:
                    if g == 0:
                        distances(b + 1, range(0, 1))
                    if g == 1:
                        reduce_extremes(b + 1)
                    if g in (0, 1):
                        for n in range(2 * C * (b + 1) + C * g, 2 * C * (b + 1) + C * (g + 1)):
                            split(n)
                    if g == 0:
                        distances(b + 1, range(1, NT))
                if g == 1 and b >= 1:
                    normalise("y", b - 1)
                if g == 2 and b + 1 < B:
                    residual(b + 1)
                if g == 3 and b + 2 < B:
                    normalise("x", b + 2)
            for n in range(B * E):
                if n == 4:
                    norm_rstd("y", B - 1)
                if 5 <= n < 5 + NT:
                    ins = norm_tile(B - 1, n - 5)
                    if n == 4 + NT:
                        ins.then_inc(norm_done, 1)
                pool.wait_ge(silu_done, n + 1)
                pool.wait_ge(in_scores[n % 3], 16 * (n // 3 + 1))
                if n >= 2:
                    pool.wait_ge(act_done, n - 1)
                pool.tensor_tensor(t1[:, n % 2, :], sg[:, n % 2, :], sbc[:, n % 3, :], ALU.mult).then_inc(t1_done, 1)

        @block.scalar
        def _(act):
            act.dma_start(npos[:, :, :], pos_cols).then_inc(in_small, 16)
            act.dma_start(bqk[:, :, :], bqk_cols).then_inc(in_bqk, 16)
            act.dma_start(tg[:, 0:1], row(g_x)).then_inc(in_gates, 16)
            act.dma_start(tg[:, 1:2], row(g_f)).then_inc(in_gates, 16)
            act.dma_start(etab[:, :, :].rearrange("p j h -> p (j h)"),
                          emb.rearrange("(o j) h -> o (j h)", o=1).broadcast_to([P, (BINS + 1) * H])).then_inc(in_tab, 16)
            act.dma_start(erow[:, :], emb_rows).then_inc(in_tab, 16)
            act.dma_start(nthr_sb[:, :], nthr.broadcast_to([P, BINS + 1])).then_inc(in_tab, 16)
            act.dma_start(slot_of[:, :], slots.broadcast_to([P, P])).then_inc(in_tab, 16)
            act.dma_start(gate_sb[:, :, :], gate_t.rearrange("(c p) e -> p c e", p=P)).then_inc(in_tab, 16)
            act.dma_start(bo_sb[:, :], row(bo)).then_inc(in_tab, 16)
            act.dma_start(wv_sb[:, :, :], wv.rearrange("(c p) n -> p c n", p=P)).then_inc(in_vow, 16)
            act.dma_start(bv_sb[:, :], row(bv)).then_inc(in_vow, 16)
            act.wait_ge(wo_zero, 1)
            for j in range(G):
                act.dma_start(wo_sb[32 * j:32 * j + HD, :, :],
                              wo.rearrange("(g j d) n -> j d g n", g=NG, j=G)[j]).then_inc(in_vow, 16)
            act.wait_ge(in_gates, 32)
            nc.scalar.activation(tg[:, :], tg[:, :], ACT.Tanh).then_inc(tg_done, 1)
            act.wait_ge(in_small, 16)
            nc.scalar.mul(npos[:, :, :], npos[:, :, :], -1.0).then_inc(npos_done, 1)
            act.wait_ge(npos_done, 1)

            def square(n, a):
                if a == 0:
                    act.wait_ge(in_pos, 16 * (n // NT + 1))
                    if n >= 2:
                        act.wait_ge(d2_sum, n - 1)
                v = pos_sb[:, :].rearrange("p (s a) -> p a s", a=3)
                if a < 3:
                    ins = nc.scalar.activation(sq[:, n % 2, a, :], v[:, a, :], ACT.Square, bias=npos[:, n, a:a + 1])
                    if a == 2:
                        ins.then_inc(sq_neg, 1)
                else:
                    act.wait_ge(sq_neg, n + 1)
                    nc.scalar.mul(sq[:, n % 2, 2, :], sq[:, n % 2, 2, :], -1.0).then_inc(sq_done, 1)

            def router_exp(b):
                act.wait_ge(lg_done, b + 1)
                nc.scalar.activation(pe[:, :, 0:E], lg[:, :, :], ACT.Exp, scale=1.0 / (XS * WS)).then_inc(lgexp_done, 1)

            def projected(kind, b):
                w = RING[kind, b]
                act.wait_ge(w_full, w + 1)
                t = W[w % 2]
                if kind == "xT":
                    nc.scalar.copy(xnT[:, :, :].rearrange("p c s -> p (c s)"), t[:, :]).then_inc(w_free[w % 2], 1)
                elif kind == "nT":
                    nc.scalar.copy(x2T[:, 0, :, b * S:(b + 1) * S],
                                   t[:, :].rearrange("p (c s) -> p c s", c=C)).then_inc(x2h_done, 1)
                else:
                    i = "kq".index(kind)
                    if b == 0 and i == 0:
                        act.wait_ge(in_bqk, 16)
                        nc.scalar.mul(bqk[:, 1, :], bqk[:, 1, :], QSCALE).then_inc(bq_scaled, 1)
                        act.wait_ge(bq_scaled, 1)
                    for c in range(C):
                        n = 2 * C * b + C * i + c
                        if n >= 2:
                            act.wait_ge(parts_done, n - 1)
                        nc.scalar.activation(qk32[:, n % 2, :], t[:, c * S:(c + 1) * S], ACT.Identity,
                                             bias=bqk[:, i, c:c + 1], scale=(1.0, QSCALE)[i]).then_inc(qk_full, 1)
                    act.wait_ge(qk_full, 2 * C * b + C * (i + 1))
                    act.sem_inc(w_free[w % 2], 1)

            def split_high_w13(e):
                act.wait_ge(in_raw[e % 2], 48 * (e // 2 + 1))
                if e == 8:
                    act.wait_ge(step_done, STEPS)
                nc.scalar.activation(w13(e)[:, 0, :, :], raw[:, e % 2, 0:2 * D].rearrange("p (m i) -> p m i", i=P),
                                     ACT.Copy, scale=WS).then_inc(w13_high, 1)

            def split_high_w2(e):
                if e == 0:
                    act.wait_ge(pv_done, STEPS * NT)
                nc.scalar.activation(w2s[:, e, 0, :], raw[:, e % 2, 2 * D:3 * D], ACT.Copy, scale=WS).then_inc(w2_high, 1)

            for kind, tile in (("k", 0), ("", 1), ("xT", None), ("q", 2), ("", 3)):
                if kind:
                    projected(kind, 0)
                if tile is not None:
                    for a in range(4):
                        square(tile, a)
            for s in range(STEPS):
                b, g = divmod(s, NG)
                for unit, e in step_units(s, 0) + step_units(s, 1):
                    if unit == "x":
                        for kind, xb in extras(s, e):
                            if kind in BY_ACT or kind == "nT":
                                projected(kind, xb)
                    if unit != "e":
                        continue
                    n = s * NE + e
                    act.wait_ge(qk_done, n + 1)
                    act.wait_ge(granted, n + 1)
                    if n >= NP_RING:
                        act.wait_ge(pv_done, (n - NP_RING) // G + 1)
                    nc.scalar.activation(pr[:, n % NP_RING, :], SC[n % 3][:, :], ACT.Exp).then_inc(exp_done, 1)
                    if s == STEPS - 2 and e in (4, 9):
                        split_high_w13(e // 5)
                    if g == 0 and b + 1 < B:
                        square((b + 1) * NT + e // 4, e % 4)
                    if g == 3 and b >= 1 and e == 1:
                        router_exp(b - 1)

            split_high_w2(0)
            split_high_w2(1)
            for n in range(B * E):
                for kind, b in LATE.get(n - 1, []):
                    if kind == "nT":
                        projected(kind, b)
                w = RING["gu", n]
                act.wait_ge(w_full, w + 1)
                if n >= 2:
                    act.wait_ge(t1_done, n - 1)
                nc.scalar.activation(sg[:, n % 2, :], W[w % 2][:, 0:S], ACT.Silu, scale=1.0 / (XS * WS)).then_inc(silu_done, 1)
                if n + 2 < E:
                    split_high_w13(n + 2)
                    split_high_w2(n + 2)
                if n == 14:
                    router_exp(B - 1)

        @block.vector
        def _(dve):
            links, w, norms = [0], [0], [0]

            def link(ins):
                links[0] += 1
                ins.then_inc(dve_chain, 1)
                dve.wait_ge(dve_chain, links[0])

            def slot():
                dve.wait_ge(w_full, w[0] + 1)
                return W[w[0] % 2]

            def used(ins):
                ins.then_inc(w_free[w[0] % 2], 1)
                w[0] += 1

            def norm_stats(b):
                if norms[0]:
                    dve.wait_ge(norm_done, norms[0])
                norms[0] += 1
                for t in range(NT):
                    ins = dve.bn_stats(st[:, t, :], x_sb[:, b * NT + t, :])
                link(ins)
                for t in range(NT):
                    ins = dve.bn_aggr(mv[:, t, :], st[:, t, :])
                link(ins)
                dve.tensor_scalar(veps[:, :], mv[:, :, 1], EPS, None, ALU.add).then_inc(veps_done, 1)

            def extremes(b, tiles):
                for r in tiles:
                    dve.wait_ge(d2_done, NT * b + r + 1)
                    ins = dve.max(m8[:, r, :], d2[:, b % 2, r, :])
                if NT - 1 not in tiles:
                    return
                if b:
                    dve.wait_ge(extr_done, b)
                link(ins)
                dve.tensor_scalar(nf[:, 0:NT], m8[:, :, 0], -NEAR, None, ALU.is_gt).then_inc(nf_done, 1)
                dve.tensor_reduce(ext[:, 0:1], m8[:, :, 0], AX.X, ALU.max)
                link(dve.scalar_tensor_tensor(out=near8[:, :, :], in0=m8[:, :, :], scalar=-NEAR, in1=m8[:, :, :],
                                              op0=ALU.is_gt, op1=ALU.mult))
                dve.tensor_reduce(ext[:, 1:2], near8[:, :, :], AX.XY, ALU.min, negate=True).then_inc(ext_done, 1)

            many = {}

            def choose_slots(b, t):
                link(dve.tensor_scalar(few[:, 0:1], t[:, NT:NT + 1], NSLOT + 0.5, None, ALU.is_lt))
                link(dve.tensor_scalar(few[:, 1:2], few[:, 0:1], 1.0, None, ALU.is_lt))
                dve.tensor_copy(flags[:, b, 0:1], few[:, 1:2])
                link(dve.tensor_scalar(nslot[:, :], nf[:, 0:NT], few[:, 0:1], None, ALU.mult))
                link(dve.scalar_tensor_tensor(out=nslot[:, :], in0=t[:, 0:NT], scalar=1.0, in1=nslot[:, :],
                                              op0=ALU.add, op1=ALU.mult))
                dve.tensor_tensor(sel.rearrange("p (t n) -> p t n", t=NT), nslot[:, :, None].broadcast_to([P, NT, P]),
                                  slot_of[:, None, :].broadcast_to([P, NT, P]), ALU.is_equal).then_inc(sel_done, 1)

            def near_rows(b, t):
                dve.wait_ge(extr_done, b + 1)
                if b:
                    dve.wait_ge(rows_out, 32 * b)
                dve.tensor_scalar(flags_f[:, 1:2], extr[:, 0:1], -NEAR, None, ALU.is_gt)
                link(dve.tensor_scalar(extr[:, 1:2], extr[:, 1:2], -1.0, None, ALU.mult))
                for i in range(2):
                    link(dve.tensor_scalar(cmp_[:, :], nthr_sb[:, 1:BINS + 1], extr[:, i:i + 1], None, ALU.is_ge))
                    link(dve.tensor_reduce(flags_f[:, 2 + i:3 + i], cmp_[:, :], AX.X, ALU.add))
                link(dve.tensor_copy(flags[:, b, 1:4], flags_f[:, 1:4]))
                dve.tensor_copy(selT, t[:, S:2 * S])
                many[b], any_ = (dve.value_load(flags[0:1, b, i:i + 1], min_val=0, max_val=1) for i in range(2))
                with dve.If(any_ > 0):
                    lo, hi = (dve.value_load(flags[0:1, b, i:i + 1], min_val=0, max_val=BINS) for i in (2, 3))
                    dist = t[:, 0:S]
                    dve.tensor_scalar(brow, dist, -NEAR, drow[:, bass.ds(hi, 1)], ALU.is_gt, ALU.mult)
                    dve.drain()
                    with dve.If(hi > lo):
                        with dve.Fori(lo + 1, hi + 1) as j:
                            dve.tensor_scalar(btmp, dist, nthr_sb[:, bass.ds(j, 1)], grow[:, bass.ds(j, 1)],
                                              ALU.is_gt, ALU.mult)
                            dve.drain()
                            dve.tensor_tensor(brow, brow, btmp, ALU.add)
                            dve.drain()
                    split_parts(nparts, brow)
                dve.drain().then_inc(rows_done, 1)

            def split_parts(out, v):
                for i in range(PARTS):
                    dve.tensor_copy(out[:, i, :], v)
                    dve.drain()
                    if i + 1 < PARTS:
                        dve.tensor_tensor(v, v, out[:, i, :], ALU.subtract)
                        dve.drain()

            def correct(tile, b, r, h):
                dist = d2[:, b % 2, r, :]
                with dve.Fori(1, BINS + 1) as j:
                    dve.tensor_scalar(btmp, dist, nthr_sb[:, bass.ds(j, 1)], gtab[:, bass.ds(j * H + h, 1)],
                                      ALU.is_gt, ALU.mult)
                    dve.drain()
                    dve.tensor_tensor(tile, tile, btmp, ALU.add)
                    dve.drain()

            def row_max(s, qt, pair, tile):
                h = G * (s % NG) + 2 * pair
                return dve.tensor_reduce(mneg[:, h:h + 2, qt], tile[:, :].rearrange("p (h k) -> p h k", h=2), AX.X, ALU.max, negate=True)

            def exp_tile(s, e):
                b, g = divmod(s, NG)
                n = s * NE + e
                dve.wait_ge(qk_done, n + 1)
                correct(SC[n % 3][:, :], b, e // G, e % G + G * g)
                dve.drain().then_inc(granted, 1)

            def max_slot(s, m, near):
                b, g = divmod(s, NG)
                t = slot()
                if near:
                    with dve.If(many[b] > 0):
                        for h in range(2):
                            correct(t[:, h * S:(h + 1) * S], b, m // 2, G * g + 2 * (m % 2) + h)
                used(row_max(s, m // 2, m % 2, t))

            def grant(s):
                with dve.If(many[s // NG] < 1):
                    dve.sem_inc(granted, NE)

            def tiles(s, half, near):
                for kind, i in step_units(s, half):
                    if kind == "x":
                        if s >= 0 and i != NM // 2:
                            for what, b in extras(s, i):
                                extra(what, b)
                        between(s, i)
                    if kind == "m":
                        max_slot(*i, near)
                    if kind == "e" and near:
                        with dve.If(many[s // NG] > 0):
                            exp_tile(s, i)

            def units(s, half):
                b, nb = max(s, 0) // NG, min(s + 1 + half, STEPS - 1) // NG
                start = w[0], links[0], norms[0]
                with dve.If(many[b] + many[nb] > 0):
                    tiles(s, half, True)
                after = w[0], links[0], norms[0]
                w[0], links[0], norms[0] = start
                with dve.Else():
                    tiles(s, half, False)
                assert after == (w[0], links[0], norms[0])

            def step(s):
                units(s, 0)
                if s + 1 < STEPS:
                    dve.drain().then_inc(m_done, 1)
                    max_parts(s + 1)
                for what, b in extras(s, NM // 2):
                    extra(what, b)
                units(s, 1)
                if 0 <= s < STEPS - 1:
                    grant(s + 1)
                dve.drain().then_inc(step_done, 1)

            def split_low_w13(e):
                dve.wait_ge(w13_high, e + 1)
                dve.scalar_tensor_tensor(out=w13(e)[:, 1, :, :].rearrange("p m i -> p (m i)"), in0=raw[:, e % 2, 0:2 * D],
                                         scalar=WS, in1=w13(e)[:, 0, :, :].rearrange("p m i -> p (m i)"),
                                         op0=ALU.mult, op1=ALU.subtract).then_inc(w13_low, 1)

            def split_low_w2(e):
                dve.wait_ge(w2_high, e + 1)
                dve.scalar_tensor_tensor(out=w2s[:, e, 1, :], in0=raw[:, e % 2, 2 * D:3 * D], scalar=WS,
                                         in1=w2s[:, e, 0, :], op0=ALU.mult, op1=ALU.subtract).then_inc(w2_low, 1)

            def between(s, place):
                b, g = divmod(s, NG)
                if s < 0:
                    return
                if s == 0 and place == 0:
                    dve.wait_ge(in_x[1], 16)
                    norm_stats(1)
                if g == 3 and place == 4 and b + 2 < B:
                    dve.wait_ge(in_x[b + 2], 16)
                    norm_stats(b + 2)
                if g == 0 and place == 6 and b:
                    dve.wait_ge(*freed(RING["wo", b - 1]))
                    norm_stats(b - 1)
                if g == 3 and place == 2 and b:
                    router(b - 1)
                if s == STEPS - 2 and place in (3, 6):
                    split_low_w13(place // 3 - 1)
                if place == 1 and s >= 1:
                    norm_out(s - 1)
                if g == 1 and b + 1 < B and place in (1, 2):
                    extremes(b + 1, (2 * place - 2, 2 * place - 1))

            def max_parts(s):
                g = s % NG
                t = slot()[0:H, 0:P]
                link(dve.tensor_copy(mpart[:, g, 0, :], t))
                for i in range(1, PARTS):
                    link(dve.tensor_tensor(mtmp[:, :], t if i == 1 else mtmp[:, :], mpart[:, g, i - 1, :], ALU.subtract))
                    if i + 1 < PARTS:
                        link(dve.tensor_copy(mpart[:, g, i, :], mtmp[:, :]))
                dve.tensor_copy(mpart[:, g, PARTS - 1, :], mtmp[:, :]).then_inc(m_split, 1)
                used(dve.drain())

            def norm_out(s):
                dve.wait_ge(pv_done, NT * (s + 1))
                q3 = rec[:, :].rearrange("p (q d) -> p q d", d=32)
                link(dve.transpose(rec[:, :], O[:, :]))
                link(dve.reciprocal(rs[:, :], q3[:, :, HD]))
                link(dve.tensor_tensor(q3, q3, rs[:, :, None].broadcast_to([P, S // 32, 32]), ALU.mult))
                dve.transpose(oT[:, s % NG, :], rec[:, :]).then_inc(oT_done, 1)
                dve.wait_ge(oT_done, s + 1)

            def router(b):
                def per_token(v):
                    return v[:, :, None].broadcast_to([P, NT, E])

                dve.wait_ge(lgexp_done, b + 1)
                p_ = pe[:, :, 0:E]
                link(dve.tensor_reduce(r4[:, :], p_, AX.X, ALU.add))
                link(dve.reciprocal(r4[:, :], r4[:, :]))
                link(dve.tensor_tensor(p_, p_, per_token(r4), ALU.mult))
                for t in range(NT):
                    ins = dve.max(top[:, t, :], pe[:, t, 0:E])
                link(ins)
                link(dve.memset(top[:, :, TOPK:8], -1.0))
                for t in range(NT):
                    ins = dve.match_replace(mr[:, t, :], top[:, t, :], pe[:, t, :], -2.0)
                link(ins)
                link(dve.scalar_tensor_tensor(out=score[:, :, :], in0=mr[:, :, 0:E], scalar=-1.5, in1=p_,
                                              op0=ALU.is_lt, op1=ALU.mult))
                link(dve.tensor_reduce(r4[:, :], score[:, :, :], AX.X, ALU.add))
                link(dve.reciprocal(r4[:, :], r4[:, :]))
                link(dve.tensor_scalar(r4[:, :], r4[:, :], tg[:, 1:2], None, ALU.mult))
                dve.tensor_tensor(score[:, :, :], score[:, :, :], per_token(r4), ALU.mult).then_inc(score_done, 1)

            def extra(kind, b):
                if kind in BY_ACT:
                    w[0] += 1
                    return
                if kind == "sc" and b:
                    dve.wait_ge(sc_out, 16 * b)
                t = slot()
                if kind == "rk":
                    choose_slots(b, t)
                    used(dve.drain())
                elif kind == "nr":
                    near_rows(b, t)
                    used(dve.drain())
                elif kind == "v":
                    dve.wait_ge(pv_done, NT * NG * b) if b else dve.wait_ge(ones_set, 1)
                    used(dve.tensor_tensor(V[:, :, 0:HD].rearrange("p (t h) d -> p t h d", t=NT),
                                           t[:, :].rearrange("p (t h d) -> p t h d", t=NT, h=H),
                                           bv_sb[:, :].rearrange("p (o h d) -> p o h d", o=1, h=H).broadcast_to([P, NT, H, HD]),
                                           ALU.add))
                elif kind == "wo":
                    dve.wait_ge(xb_done, b + 1)
                    xs = x_sb[:, b * NT:(b + 1) * NT, :].rearrange("p t d -> p (t d)")
                    used(dve.scalar_tensor_tensor(out=xs, in0=t[:, :], scalar=tg[:, 0:1], in1=xs,
                                                  op0=ALU.mult, op1=ALU.add))
                elif kind == "nT":
                    cols = slice(b * S, (b + 1) * S)
                    t3 = t[:, :].rearrange("p (c s) -> p c s", c=C)
                    dve.wait_ge(x2h_done, b + 1)
                    used(dve.tensor_tensor(x2T[:, 1, :, cols], t3, x2T[:, 0, :, cols], ALU.subtract))
                elif kind == "lg":
                    t3 = t[:, 0:NT * E].rearrange("p (t e) -> p t e", t=NT)
                    link(dve.tensor_reduce(r4[:, :], t3, AX.X, ALU.max))
                    dve.tensor_tensor(lg[:, :, :], t3, r4[:, :, None].broadcast_to([P, NT, E]),
                                      ALU.subtract).then_inc(lg_done, 1)
                    used(dve.drain())
                elif kind == "sc":
                    dve.tensor_copy(scT[:, :], t[0:E, 0:S]).then_inc(scT_done, 1)
                    used(dve.drain())

            dve.wait_ge(in_x[0], 16)
            norm_stats(0)
            dve.memset(Kst[ROWS:P, :, :].rearrange("p h s -> p (h s)").bitcast(F32), TWO_ONES)
            dve.wait_ge(rstd_done, 1)
            for t in range(NT):
                ins = dve.tensor_scalar(xn[:, t, :], x_sb[:, t, :], mv[:, t, 0:1], rstd[:, t:t + 1],
                                        ALU.subtract, ALU.mult)
            ins.then_inc(norm_done, 1)
            dve.wait_ge(in_tab, 16 * 6)
            dve.wait_ge(tg_done, 1)
            dve.wait_ge(idents, 1)
            dve.memset(top[:, :, :], -1.0)
            link(dve.tensor_tensor(dtab[:, :].rearrange("p (j h) -> p j h", h=H), etab[:, :, :],
                                   etab[:, BINS:BINS + 1, :].broadcast_to([P, BINS + 1, H]), ALU.subtract))
            dve.tensor_tensor(gtab[:, H:], etab[:, 0:BINS, :].rearrange("p j h -> p (j h)"),
                              etab[:, 1:BINS + 1, :].rearrange("p j h -> p (j h)"), ALU.subtract)
            dve.tensor_scalar(drow[:, :], erow[:, :], erow[:, BINS:BINS + 1], None, ALU.subtract)
            dve.tensor_tensor(grow[:, 1:], erow[:, 0:BINS], erow[:, 1:BINS + 1], ALU.subtract)
            dve.tensor_scalar(bo_sb[:, :], bo_sb[:, :], tg[:, 0:1], None, ALU.mult).then_inc(tabs_done, 1)
            for kind, b in extras(-1, 0):
                if kind == "rk":
                    for n in range(2 * C):
                        dve.wait_ge(qk_full, n + 1)
                        if n >= 2:
                            dve.wait_ge(parts_out[n % 2], 16 * (n // 2))
                        split_parts(parts[:, n % 2, :, :], qk32[:, n % 2, :])
                        dve.drain().then_inc(parts_done, 1)
                    extremes(0, range(NT))
                if kind == "nr":
                    for h in range(H):
                        ins = dve.tensor_scalar(diag[:, 0, h, :], ident[:, :], dtab[:, h:h + 1], None, ALU.mult)
                    link(ins)
                    for h in range(H):
                        dve.scalar_tensor_tensor(out=diag[:, 1, h, :], in0=ident[:, :], scalar=dtab[:, h:h + 1],
                                                 in1=diag[:, 0, h, :], op0=ALU.mult, op1=ALU.subtract)
                    link(dve.tensor_scalar(gate_h[:, 0, :, :], gate_sb[:, :, :], WS, None, ALU.mult))
                    dve.scalar_tensor_tensor(out=gate_h[:, 1, :, :], in0=gate_sb[:, :, :], scalar=WS, in1=gate_h[:, 0, :, :],
                                             op0=ALU.mult, op1=ALU.subtract).then_inc(tabs_done, 1)
                extra(kind, b)
            grant(0)
            step(-1)
            dve.wait_ge(in_vow, 16 * 6)
            for s in range(STEPS):
                step(s)

            def result(b):
                dve.wait_ge(w2_used, E * (b + 1))
                if b:
                    dve.wait_ge(out_done, 16 * b)
                for c in range(C):
                    ins = dve.tensor_scalar(osb[:, c, :], Y[b % 2][c][:, :], 1.0 / WS, None, ALU.mult)
                ins.then_inc(osb_done, 1)

            norm_out(STEPS - 1)
            split_low_w2(0)
            split_low_w2(1)
            for n in range(B * E):
                t = slot()
                dve.wait_ge(t1_done, n + 1)
                used(dve.scalar_tensor_tensor(out=ac[:, n % 2, :], in0=t[:, S:2 * S], scalar=1.0 / (XS * WS),
                                              in1=t1[:, n % 2, :], op0=ALU.mult, op1=ALU.mult))
                dve.wait_ge(*freed(w[0] - 1))
                if n >= 3:
                    dve.wait_ge(w2_used, n - 2)
                link(dve.tensor_copy(ahl[:, n % 3, 0, :], ac[:, n % 2, :]))
                dve.tensor_tensor(ahl[:, n % 3, 1, :], ac[:, n % 2, :], ahl[:, n % 3, 0, :], ALU.subtract).then_inc(act_done, 1)
                if n + 2 < E:
                    split_low_w13(n + 2)
                    split_low_w2(n + 2)
                for kind, b in LATE.get(n, []):
                    extra(kind, b)
                if n == 3:
                    dve.wait_ge(*freed(RING["wo", B - 1]))
                    norm_stats(B - 1)
                if n == 15:
                    router(B - 1)
                if n % E == 2 and n >= E:
                    result(n // E - 1)
            result(B - 1)

        @block.tensor
        def _(pe_):
            mm, w, o_n = nc.tensor.matmul, [0], [0]

            def slot():
                if w[0] >= 2:
                    pe_.wait_ge(*freed(w[0] - 2))
                return W[w[0] % 2]

            def full(ins):
                w[0] += 1
                ins.then_inc(w_full, 1)

            def transposes(t):
                for c in range(C):
                    for k in range(NT):
                        ins = nc.tensor.transpose(t[:, c * S + k * P:c * S + (k + 1) * P], xn[:, k, c * P:(c + 1) * P],
                                                  ident[:, :])
                full(ins)

            def extra(kind, b):
                if kind == "xT":
                    pe_.wait_ge(norm_done, NORM["x", b] + 1)
                elif kind == "q":
                    pe_.wait_ge(*freed(RING["xT", b]))
                elif kind == "k":
                    pe_.wait_ge(in_ctx, 16 * (b + 1))
                    if b == 0:
                        pe_.wait_ge(in_qkw, 32)
                elif kind == "v" and b == 0:
                    pe_.wait_ge(in_vow, 16 * 6)
                elif kind == "wo":
                    pe_.wait_ge(oT_done, NG * (b + 1))
                elif kind == "nT":
                    pe_.wait_ge(norm_done, NORM["y", b] + 1)
                elif kind == "lg":
                    pe_.wait_ge(*freed(RING["nT", b]))
                    pe_.wait_ge(tabs_done, 2)
                elif kind == "sc":
                    pe_.wait_ge(score_done, b + 1)
                elif kind == "rk":
                    pe_.wait_ge(nf_done, b + 1)
                elif kind == "nr":
                    pe_.wait_ge(sel_done, b + 1)
                t = slot()
                if kind == "rk":
                    mm(t[:, 0:NT + 1], before[:, :], nf[:, :], start=True, stop=False, skip_group_check=True)
                    for i in range(1, NT + 1):
                        ins = mm(t[:, i:NT + 1], ones[:, :], nf[:, 0:NT + 1 - i], start=False, stop=(i == NT),
                                 skip_group_check=True)
                    full(ins)
                elif kind == "nr":
                    for k in range(NT):
                        mm(t[:, 0:S], sel[:, k * P:(k + 1) * P], d2[:, b % 2, k, :], start=(k == 0), stop=(k == NT - 1))
                    for k in range(NT):
                        ins = nc.tensor.transpose(t[:, S + k * P:S + (k + 1) * P], sel[:, k * P:(k + 1) * P],
                                                  ident[:, :])
                    full(ins)
                elif kind == "xT" or kind == "nT":
                    transposes(t)
                elif kind == "q" or kind == "k":
                    wt, src = (wq_sb, xnT) if kind == "q" else (wk_sb, cT)
                    for c in range(C):
                        for k in range(C):
                            ins = mm(t[:, c * S:(c + 1) * S], wt[:, k, c * P:(c + 1) * P], src[:, k, :],
                                     start=(k == 0), stop=(k == C - 1))
                    full(ins)
                elif kind == "v":
                    for k in range(NT):
                        for c in range(C):
                            ins = mm(t[:, k * D:(k + 1) * D], cT[:, c, k * P:(k + 1) * P], wv_sb[:, c, :],
                                     start=(c == 0), stop=(c == C - 1))
                    full(ins)
                elif kind == "wo":
                    for k in range(NT):
                        for g in range(NG):
                            ins = mm(t[:, k * D:(k + 1) * D], oT[:, g, k * P:(k + 1) * P], wo_sb[:, g, :],
                                     start=(g == 0), stop=(g == NG - 1))
                    full(ins)
                elif kind == "lg":
                    pairs = [(c, i, j) for c in range(C) for i, j in ((0, 0), (0, 1), (1, 0))]
                    for k in range(NT):
                        for m, (c, i, j) in enumerate(pairs):
                            ins = mm(t[:, k * E:(k + 1) * E], x2T[:, i, c, b * S + k * P:b * S + (k + 1) * P],
                                     gate_h[:, j, c, :], start=(m == 0), stop=(m == len(pairs) - 1))
                    full(ins)
                elif kind == "sc":
                    for k in range(NT):
                        ins = nc.tensor.transpose(t[0:E, k * P:(k + 1) * P], score[:, k, :], ident[:, :])
                    full(ins)

            def exp_scores(s, e):
                b, g = divmod(s, NG)
                n, r, h = s * NE + e, e // G, G * g + e % G
                if e == 0:
                    pe_.wait_ge(m_in, 16 * PARTS * (s + 1))
                if n >= 3:
                    pe_.wait_ge(exp_done, n - 2)
                mm(SC[n % 3][:, :], Kst[0:KROWS, h, r * P:(r + 1) * P], Qst[0:KROWS, h, :], start=True, stop=False,
                   skip_group_check=True)
                for i in range(2):
                    ins = mm(SC[n % 3][:, r * P:(r + 1) * P], ident_h[:, :], diag[:, i, h, :], start=False,
                             stop=(i == 1), skip_group_check=True)
                ins.then_inc(qk_done, 1)

            def max_scores(s, m):
                b, g = divmod(s, NG)
                r = m // 2
                if m == 0 and g % 2 == 0:
                    pe_.wait_ge(stack_in[g // 2], 16 * STACK_DMAS * (b + 1))
                t = slot()
                for i in range(2):
                    h = G * g + 2 * (m % 2) + i
                    mm(t[:, i * S:(i + 1) * S], Qst[0:NROWS, h, r * P:(r + 1) * P], Kst[0:NROWS, h, :],
                       start=True, stop=False, skip_group_check=True)
                    ins = mm(t[:, i * S + r * P:i * S + (r + 1) * P], ident_h[:, :], diag[:, 0, h, :],
                             start=False, stop=True, skip_group_check=True)
                full(ins)

            def max_transpose(s):
                pe_.wait_ge(m_done, s + 1)
                g = s % NG
                full(nc.tensor.transpose(slot()[0:H, 0:P], mneg[:, G * g:G * g + G, :].rearrange("p h t -> p (h t)"),
                                         ident[:, :]))

            def values(s, r):
                b, g = divmod(s, NG)
                if r == 0:
                    if s:
                        pe_.wait_ge(oT_done, s)
                    if g == 0:
                        pe_.wait_ge(*freed(RING["v", b]))
                pe_.wait_ge(exp_done, s * NE + (r + 1) * G)
                for j in range(G):
                    n = s * NE + r * G + j
                    ins = mm(O[32 * j:32 * j + 32, :], V[:, r * H + G * g + j, :], pr[:, n % NP_RING, :],
                             start=(r == 0), stop=(r == NT - 1), skip_group_check=True)
                ins.then_inc(pv_done, 1)

            pe_.wait_ge(idents, 1)
            for s in range(-1, STEPS):
                late = s >= 1
                for kind, i in step_units(s, 0) + step_units(s, 1):
                    if kind == "x":
                        for what, b in extras(s, i):
                            extra(what, b)
                            if late:
                                values(s - 1, NT - 1)
                                late = False
                        if s == -1 and i == 0:
                            pe_.wait_ge(tabs_done, 2)
                            pe_.wait_ge(ones_set, 1)
                    if kind == "e":
                        exp_scores(s, i)
                        if i == 1 and late:
                            values(s - 1, NT - 1)
                            late = False
                        if i % G == 1 and i > G:
                            values(s, i // G - 1)
                    if kind == "m":
                        max_scores(*i)
                    if kind == "t":
                        max_transpose(i)

            def gate_up(n):
                b, e = divmod(n, E)
                if b == 0:
                    pe_.wait_ge(w13_low, e + 1)
                if e == 0:
                    pe_.wait_ge(*freed(RING["nT", b]))
                t = slot()
                for m in range(2):
                    pairs = [(c, i, j) for c in range(C) for i, j in ((0, 0), (0, 1), (1, 0))]
                    for k, (c, i, j) in enumerate(pairs):
                        ins = mm(t[:, m * S:(m + 1) * S], w13(e)[:, i, C * m + c, :], x2T[:, j, c, b * S:(b + 1) * S],
                                 start=(k == 0), stop=(k == len(pairs) - 1))
                full(ins)

            def down(n):
                b, e = divmod(n, E)
                pe_.wait_ge(act_done, n + 1)
                if b == 0:
                    pe_.wait_ge(w2_low, e + 1)
                if n == 0:
                    pe_.wait_ge(exp_done, EXPS)
                if n == E:
                    pe_.wait_ge(oT_done, STEPS)
                if e == 0 and b >= 2:
                    pe_.wait_ge(osb_done, b - 1)
                y = Y[b % 2]
                for c in range(C):
                    for k, (i, j) in enumerate(((0, 0), (0, 1), (1, 0))):
                        ins = mm(y[c][:, :], w2s[:, e, i, c * P:(c + 1) * P], ahl[:, n % 3, j, :],
                                 start=(e == 0 and k == 0), stop=(e == E - 1 and k == 2), skip_group_check=True)
                ins.then_inc(w2_used, 1)
                if e == 0:
                    for c in range(C):
                        for k in range(NT):
                            mm(y[c][:, k * P:(k + 1) * P], x_sb[:, b * NT + k, c * P:(c + 1) * P], ident_w[:, :],
                               start=False, stop=False, skip_group_check=True)

            values(STEPS - 1, NT - 1)
            for n in range(B * E):
                gate_up(n)
                for kind, b in LATE.get(n, []):
                    extra(kind, b)
                if n >= 2:
                    down(n - 2)
            down(B * E - 2)
            down(B * E - 1)


def kernel(**inputs):
    import concourse.bacc as bacc
    from concourse.bass_utils import run_bass_kernel_spmd

    a = {k: np.asarray(v) for k, v in inputs.items()}
    pos_ = a["fside_BxSx3_0"]
    given = {
        "x": a["x"],
        "ctx_t": a["ctx_1024"].reshape(B * S, D).T,
        "pos": pos_.reshape(B, S * 3),
        "pos_cols": pos_.reshape(B * NT, P, 3).transpose(1, 0, 2),
        "g_x": a["g_xattn"], "g_f": a["g_ffn"],
        "wq": a["L0_xattn_Wq"], "wk": a["L0_xattn_Wk"],
        "bqk_cols": np.stack([a["L0_xattn_bk"].reshape(C, P), a["L0_xattn_bq"].reshape(C, P)]).transpose(2, 0, 1),
        "wv": a["L0_xattn_Wv"], "bv": a["L0_xattn_bv"], "wo": a["L0_xattn_Wo"], "bo": a["L0_xattn_bo"],
        "emb": a["L0_xattn_dist_emb"], "emb_rows": np.tile(a["L0_xattn_dist_emb"].T, (NSLOT, 1)), "gate_t": a["L0_ffn_gate_w"].T,
        "w1": a["L0_ffn_w1"], "w3": a["L0_ffn_w3"], "w2": a["L0_ffn_w2"], "nthr": -THRESHOLDS,
        "slots": np.repeat(np.arange(1, NSLOT + 1, dtype=np.float32), H)[None, :],
    }
    nc = bacc.Bacc("TRN2", target_bir_lowering=False, num_devices=1)
    arrays, args = {}, {}
    for name, v in given.items():
        v = np.ascontiguousarray(v)
        arrays[f"in_{name}"] = v
        args[name] = nc.dram_tensor(f"in_{name}", v.shape, mybir.dt.from_np(v.dtype), kind="ExternalInput").ap()
    args["out_t"] = nc.dram_tensor("out_t", (D, B * S), F32, kind="ExternalOutput").ap()
    gated_block(nc, **args)
    got = run_bass_kernel_spmd(nc, [arrays], core_ids=[0]).results[0]["out_t"]
    return np.ascontiguousarray(got.T).reshape(B, S, D)
```

```python
from contextlib import ExitStack

import numpy as np

import concourse.bass as bass
from concourse import mybir

ALU = mybir.AluOpType
ACT = mybir.ActivationFunctionType
F32 = mybir.dt.float32
BF16 = mybir.dt.bfloat16
F16 = mybir.dt.float16
I32 = mybir.dt.int32
AX = mybir.AxisListType
RMAX = bass.bass_isa.ReduceOp.max

P = 128
B, S, D = 4, 512, 256
H, HD = 16, 16
NT = S // P
C = D // P
G = 4
NG = H // G
STEPS = B * NG
BINS = 32
FAR = 1e30
E, TOPK = 16, 4
PARTS = 3
QPART = [0, 1, 0, 1, 2, 0]
KPART = [0, 1, 2, 0, 0, 1]
NPROD = len(QPART)


def runs(order):
    out = []
    for place, part in enumerate(order):
        if out and part == out[-1][1] + out[-1][2]:
            out[-1] = (out[-1][0], out[-1][1], out[-1][2] + 1)
        else:
            out.append((place, part, 1))
    return out


ROWS = NPROD * HD
NSLOT = 8
NROWS = ROWS + PARTS * NSLOT
KROWS = NROWS + PARTS
STACK_DMAS = len(runs(QPART)) + len(runs(KPART)) + PARTS + 1
EPS = 1e-5
XS, WS = 64.0, 16.0
QSCALE = 1.0 / float(np.sqrt(HD))
NP_RING = 8
NRAW = 4
NE = G * NT
NM = 8


def step_units(s, half):
    order = []
    for i in range(half * NM // 2, (half + 1) * NM // 2):
        order.append(("x", i))
        slots = [(s + 1, NM // 2 + i)] if half == 0 else [(s + 2, i - NM // 2)]
        if s == -1 and half == 0:
            slots = [(0, 2 * i), (0, 2 * i + 1)]
        order += [("m", m) for m in slots if m[0] < STEPS]
        if s >= 0:
            order += [("e", 2 * i), ("e", 2 * i + 1)]
        if i == NM // 2 and s + 1 < STEPS:
            order.append(("t", s + 1))
    return order


def extras(s, place):
    b, g = divmod(s, NG)
    if s == -1:
        return {0: [("k", 0), ("xT", 0), ("q", 0), ("rk", 0), ("nr", 0), ("v", 0)],
                4: [("k", 1)], 5: [("xT", 1)], 7: [("q", 1)]}.get(place, [])
    prev, nxt, ahead = b >= 1, b + 1 < B, 1 <= b < B - 1
    return [(kind, c) for where, at, kind, c, there in (
        (0, 0, "v", b, prev), (0, 2, "k", b + 1, ahead),
        (1, 0, "xT", b + 1, ahead), (1, 1, "q", b + 1, ahead), (1, 3, "rk", b + 1, nxt), (1, 4, "nr", b + 1, nxt),
        (2, 0, "wo", b - 1, prev),
        (3, 3, "nT", b - 1, prev), (3, 5, "sc", b - 2, b >= 2), (3, 6, "lg", b - 1, prev),
    ) if (where, at) == (g, place) and there]


BY_ACT = ("k", "xT", "q")

LATE = {1: [("wo", B - 1)], 8: [("sc", B - 2)], 10: [("nT", B - 1)], 12: [("lg", B - 1)], 17: [("sc", B - 1)]}


def ring_order():
    order = []
    for s in range(-1, STEPS):
        for half in range(2):
            for kind, i in step_units(s, half):
                order += extras(s, i) if kind == "x" else [(kind, i)] if kind in "mt" else []
    for n in range(B * E):
        order += [("gu", n)] + LATE.get(n, [])
    return order


RING = {what: n for n, what in enumerate(ring_order())}


def norm_order():
    order = [("x", 0), ("x", 1)]
    for b in range(B):
        order += [("y", b - 1)] * (b >= 1) + [("x", b + 2)] * (b + 2 < B)
    return order + [("y", B - 1)]


NORM = {what: n for n, what in enumerate(norm_order())}


def bin_thresholds():
    def binned(d2):
        return np.float32(np.sqrt(d2)) / np.float32(5.0) * np.float32(BINS)
    out = np.zeros((1, BINS + 1), np.float32)
    for j in range(1, BINS + 1):
        t = np.float32((5.0 * j / BINS) ** 2)
        while binned(np.nextafter(t, np.float32(0))) >= j:
            t = np.nextafter(t, np.float32(0))
        while binned(t) < j:
            t = np.nextafter(t, np.float32(np.inf))
        out[0, j] = t
    return out


TWO_ONES = float(np.array([0x3F803F80], np.uint32).view(np.float32)[0])
THRESHOLDS = bin_thresholds()
NEAR = float(THRESHOLDS[0, BINS])


def gated_block(nc, x, ctx_t, pos, pos_cols, g_x, g_f, wq, wk, bqk_cols, wv, bv, wo, bo, emb, emb_rows, gate_t,
                w1, w3, w2, nthr, slots, out_t):
    q_dram = nc.dram_tensor("q_parts", (C, PARTS, P, S), BF16, kind="Internal").ap()
    k_dram = nc.dram_tensor("k_parts", (C, PARTS, P, S), BF16, kind="Internal").ap()
    nq_dram = nc.dram_tensor("near_bias", (PARTS, P, S), BF16, kind="Internal").ap()
    nk_dram = nc.dram_tensor("near_keys", (P, S), BF16, kind="Internal").ap()
    sc_dram = nc.dram_tensor("scores", (E, B * S), F32, kind="Internal").ap()

    with ExitStack() as ctx:
        def sb(name, shape, dt=F32):
            return ctx.enter_context(nc.sbuf_tensor(name, shape, dt))

        def sem(name):
            return ctx.enter_context(nc.semaphore(name))

        W = [ctx.enter_context(nc.psum_tensor(f"W{i}", [P, 1024], F32)) for i in range(2)]
        SC = [ctx.enter_context(nc.psum_tensor(f"SC{i}", [P, S], F32)) for i in range(3)]
        O = ctx.enter_context(nc.psum_tensor("O", [P, S], F32))
        Y = [[SC[0], SC[1]], [SC[2], O]]

        ident = sb("ident", [P, P])
        ident_h = sb("ident_h", [P, P], F16)
        ident_w = sb("ident_w", [P, P])
        x_sb = sb("x_sb", [P, B * NT, D])
        xn = sb("xn", [P, NT, D])
        xnT = sb("xnT", [P, C, S])
        cT = sb("cT", [P, C, S])
        x2T = sb("x2T", [P, 2, C, B * S], F16)
        wq_sb, wk_sb, wv_sb = (sb(n, [P, C, D]) for n in ("wq_sb", "wk_sb", "wv_sb"))
        wo_sb = sb("wo_sb", [P, NG // 2, D])
        bqk = sb("bqk", [P, 2, C])
        bv_sb = sb("bv_sb", [P, D])
        bo_sb = sb("bo_sb", [P, D])
        tg = sb("tg", [P, 2])
        dtab = sb("dtab", [P, (BINS + 1) * H])
        gtab = sb("gtab", [P, (BINS + 1) * H])
        erow = sb("erow", [P, BINS + 1])
        drow = sb("drow", [P, BINS + 1])
        grow = sb("grow", [P, BINS + 1])
        nthr_sb = sb("nthr_sb", [P, BINS + 1])
        slot_of = sb("slot_of", [P, P])
        before = sb("before", [P, P])
        ones = sb("ones", [P, P])
        diag = sb("diag", [P, 2, H, P], F16)
        qk32 = sb("qk32", [P, 2, S])
        parts = sb("parts", [P, 2, PARTS, S], BF16)
        Qst = sb("Qst", [P, H, S], BF16)
        Kst = sb("Kst", [P, H, S], BF16)
        V = sb("V", [P, NT * H, 2 * HD])
        mneg = sb("mneg", [P, H, NT])
        mtmp = sb("mtmp", [H, P])
        mpart = sb("mpart", [H, NG, PARTS, P], BF16)
        pr = sb("pr", [P, NP_RING, S])
        rec = sb("rec", [P, S])
        rs = sb("rs", [P, S // 32])
        opair = sb("opair", [P, S])
        oT = sb("oT", [P, NG // 2, S])
        pos_sb = sb("pos_sb", [P, S * 3])
        npos = sb("npos", [P, B * NT, 3])
        d2 = sb("d2", [P, 2, NT, S])
        m8 = sb("m8", [P, NT, 8])
        near8 = sb("near8", [P, NT, 8])
        nf = sb("nf", [P, NT + 1])
        nslot = sb("nslot", [P, NT])
        few = sb("few", [P, 2])
        ext = sb("ext", [P, 2])
        extr = sb("extr", [P, 2])
        cmp_ = sb("cmp", [P, BINS])
        flags_f = sb("flags_f", [P, 4])
        flags = sb("flags", [P, B, 4], I32)
        st = sb("st", [P, NT, 6])
        mv = sb("mv", [P, NT, 2])
        veps = sb("veps", [P, NT])
        nhalf = sb("nhalf", [P, NT])
        rstd = sb("rstd", [P, NT])
        gate_sb = sb("gate_sb", [P, C, E])
        gate_h = sb("gate_h", [P, 2, C, E], F16)
        lg = sb("lg", [P, NT, E])
        pe = sb("pe", [P, NT, E + TOPK])
        top = sb("top", [P, NT, 8])
        mr = sb("mr", [P, NT, E + TOPK])
        r4 = sb("r4", [P, NT])
        score = sb("score", [P, NT, E])
        scT = sb("scT", [E, S])
        sq = sb("sq", [P, 2, 3, S])
        w13a = sb("w13a", [P, 8 * 4 * 2 * P], F16)
        early = w13a[:, :].bitcast(F32)
        sel, brow, btmp = (early[:, i * S:(i + 1) * S] for i in (0, 1, 7))
        nparts = early[:, 3 * S:3 * S + PARTS * S // 2].bitcast(BF16).rearrange("p (a s) -> p a s", a=PARTS)
        etab = early[:, 11 * S // 2:11 * S // 2 + (BINS + 1) * H].rearrange("p (j h) -> p j h", h=H)
        selT = early[:, 5 * S:5 * S + S // 2].bitcast(BF16)
        raw = sq[:, :, :, :].rearrange("p i a s -> p (i a s)").rearrange("p (n m) -> p n m", n=NRAW)
        w13b = d2[:, :, :, :].rearrange("p a t s -> p (a t s)").bitcast(F16)
        w2s = pr[:, :, :].rearrange("p n s -> p (n s)").bitcast(F16).rearrange(
            "p (e l n) -> p e l n", e=E, l=2)

        def w13(e):
            t = w13a[:, :] if e < 8 else w13b
            return t.rearrange("p (e l m i) -> p e l m i", e=8, l=2, m=4)[:, e % 8]

        over_q = Qst[:, :, :].rearrange("p h s -> p (h s)").bitcast(F32)
        sg, t1, ac = (over_q[:, i * 2 * S:(i + 1) * 2 * S].rearrange("p (n s) -> p n s", n=2) for i in range(3))
        over_k = Kst[:, :, :].rearrange("p h s -> p (h s)").bitcast(F32)
        sbc = over_k[:, 0:3 * S].rearrange("p (n s) -> p n s", n=3)
        ahl = over_k[:, 3 * S:6 * S].bitcast(F16).rearrange("p (n l s) -> p n l s", n=3, l=2)
        osb = qk32

        in_x = [sem(f"in_x{b}") for b in range(B)]
        stack_in = [sem(f"stack_in{g}") for g in range(NG)]
        in_ctx, in_pos, in_wk, in_wq, in_bqk, in_vow = (sem(n) for n in "in_ctx in_pos in_wk in_wq in_bqk in_vow".split())
        in_small, in_gates, in_tab = (sem(n) for n in "in_small in_gates in_tab".split())
        in_raw = [sem(f"in_raw{i}") for i in range(NRAW)]
        in_scores = [sem(f"in_scores{i}") for i in range(3)]
        w_full, w_free = sem("w_full"), [sem(f"w_free{i}") for i in range(2)]
        idents, ones_set, tabs_done, tg_done, npos_done = (
            sem(n) for n in "idents ones_set tabs_done tg_done npos_done".split())
        veps_done, rstd_done, norm_done, xb_done, x2h_done, bq_scaled = (
            sem(n) for n in "veps_done rstd_done norm_done xb_done x2h_done bq_scaled".split())
        qk_full, parts_done = (sem(n) for n in "qk_full parts_done".split())
        parts_out = [sem(f"parts_out{i}") for i in range(2)]
        sq_done, d2_sum, d2_done, ext_done, extr_done, step_done = (
            sem(n) for n in "sq_done d2_sum d2_done ext_done extr_done step_done".split())
        m_done, m_split, m_in, qk_done, granted, exp_done, pv_done = (
            sem(n) for n in "m_done m_split m_in qk_done granted exp_done pv_done".split())
        oT_done, lg_done, lgexp_done, score_done, scT_done, sc_out = (
            sem(n) for n in "oT_done lg_done lgexp_done score_done scT_done sc_out".split())
        w13_high, w13_low, w2_high, w2_low, silu_done, t1_done, act_done, w2_used = (
            sem(n) for n in "w13_high w13_low w2_high w2_low silu_done t1_done act_done w2_used".split())
        osb_done, out_done = sem("osb_done"), sem("out_done")
        nf_done, sel_done, brow_zero, brow_done, rows_done, rows_out = (
            sem(n) for n in "nf_done sel_done brow_zero brow_done rows_done rows_out".split())
        sq_neg, o_read = sem("sq_neg"), sem("o_read")
        dve_chain, pool_chain = sem("dve_chain"), sem("pool_chain")

        block = ctx.enter_context(nc.Block())
        EXPS = STEPS * NE

        def freed(n):
            return w_free[n % 2], n // 2 + 1

        def row(ap):
            return ap.rearrange("(o n) -> o n", o=1).broadcast_to([P, ap.shape[0]])

        @block.sync
        def _(sp):
            def load_x(b):
                sp.dma_start(x_sb[:, b * NT:(b + 1) * NT, :],
                             x[b].rearrange("(t p) d -> p t d", p=P)).then_inc(in_x[b], 16)

            def load_ctx(b):
                if b:
                    sp.wait_ge(w_full, RING["v", b - 1] + 1)
                sp.dma_start(cT[:, :, :], ctx_t[:, b * S:(b + 1) * S].rearrange("(c p) s -> p c s", p=P)
                             ).then_inc(in_ctx, 16)

            def load_pos(b):
                sp.wait_ge(sq_done, NT * b)
                sp.dma_start(pos_sb[:, :], pos[b:b + 1, :].broadcast_to([P, S * 3])).then_inc(in_pos, 16)

            def store_parts(b, which):
                if b:
                    sp.wait_ge(stack_in[NG - 1], 16 * STACK_DMAS * b)
                for i in which:
                    n = 2 * C * b + i
                    sp.wait_ge(parts_done, n + 1)
                    sp.dma_start((q_dram if i >= C else k_dram)[i % C].rearrange("a p s -> p a s"),
                                 parts[:, n % 2, :, :]).then_inc(parts_out[n % 2], 16)

            def store_rows(b):
                sp.wait_ge(rows_done, b + 1)
                sp.dma_start(nk_dram, selT).then_inc(rows_out, 16)
                sp.dma_start(nq_dram.rearrange("a p s -> p a s"), nparts).then_inc(rows_out, 16)

            def load_stack(b, g, which):
                for out in parts_out:
                    sp.wait_ge(out, 16 * (C * b + which + 1))
                if b:
                    sp.wait_ge(qk_done, NE * ((b - 1) * NG + g + 1))
                stack, dram, order = ((Kst, k_dram, KPART), (Qst, q_dram, QPART))[which]
                c, h = divmod(G * g, H // C)
                for place, first, count in runs(order):
                    sp.dma_start(stack[place * HD:(place + count) * HD, G * g:G * g + G, :],
                                 dram[c, first:first + count].rearrange("a (d h) s -> (a d) h s", d=HD)[:, h:h + G, :]
                                 ).then_inc(stack_in[g], 16)

            def load_rows(b, g):
                sp.wait_ge(rows_out, 32 * (b + 1))
                for i in range(PARTS):
                    sp.dma_start(Kst[ROWS + i * NSLOT:ROWS + (i + 1) * NSLOT, G * g:G * g + G, :],
                                 nk_dram.rearrange("(n h) s -> n h s", h=H)[:, G * g:G * g + G, :]
                                 ).then_inc(stack_in[g], 16)
                sp.dma_start(Qst[ROWS:NROWS, G * g:G * g + G, :],
                             nq_dram.rearrange("a (n h) s -> (a n) h s", h=H)[:, G * g:G * g + G, :]
                             ).then_inc(stack_in[g], 16)

            def load_group(b, g):
                load_stack(b, g, 0)
                load_stack(b, g, 1)
                load_rows(b, g)

            def load_max_rows(s):
                g = s % NG
                sp.wait_ge(m_split, s + 1)
                for i in range(PARTS):
                    sp.dma_start(Qst[NROWS + i:NROWS + i + 1, G * g:G * g + G, :].rearrange(
                        "o h (t q) -> o (h t) q", q=P), mpart[:, g, i, :]).then_inc(m_in, 16)

            def store_scores(b):
                sp.wait_ge(scT_done, b + 1)
                sp.dma_start(sc_dram[:, b * S:(b + 1) * S], scT[:, :]).then_inc(sc_out, 16)

            def load_expert(e):
                if e >= NRAW:
                    sp.wait_ge(w2_low, e - NRAW + 1)
                if e == 0:
                    sp.wait_ge(d2_sum, NT * B)
                r = raw[:, e % NRAW, :]
                for i, w in enumerate((w1, w3)):
                    sp.dma_start(r[:, i * D:(i + 1) * D].rearrange("p (c i) -> p c i", c=C),
                                 w[e].rearrange("(c p) i -> p c i", p=P)).then_inc(in_raw[e % NRAW], 16)
                sp.dma_start(r[:, 2 * D:3 * D], w2[e]).then_inc(in_raw[e % NRAW], 16)

            load_ctx(0)
            load_x(0)
            for w, t, done in ((wk, wk_sb, in_wk), (wq, wq_sb, in_wq)):
                sp.dma_start(t[:, :, :], w.rearrange("(c p) n -> p c n", p=P)).then_inc(done, 16)
            sp.dma_start(tg[:, 0:1], row(g_x)).then_inc(in_gates, 16)
            sp.dma_start(tg[:, 1:2], row(g_f)).then_inc(in_gates, 16)
            sp.dma_start(etab[:, :, :].rearrange("p j h -> p (j h)"),
                         emb.rearrange("(o j) h -> o (j h)", o=1).broadcast_to([P, (BINS + 1) * H])).then_inc(in_tab, 16)
            sp.dma_start(erow[:, :], emb_rows).then_inc(in_tab, 16)
            sp.dma_start(nthr_sb[:, :], nthr.broadcast_to([P, BINS + 1])).then_inc(in_tab, 16)
            sp.dma_start(slot_of[:, :], slots.broadcast_to([P, P])).then_inc(in_tab, 16)
            sp.dma_start(gate_sb[:, :, :], gate_t.rearrange("(c p) e -> p c e", p=P)).then_inc(in_tab, 16)
            sp.dma_start(bo_sb[:, :], row(bo)).then_inc(in_tab, 16)
            sp.dma_start(wv_sb[:, :, :], wv.rearrange("(c p) n -> p c n", p=P)).then_inc(in_vow, 16)
            sp.dma_start(bv_sb[:, :], row(bv)).then_inc(in_vow, 16)
            sp.dma_start(wo_sb[:, :, :], wo).then_inc(in_vow, 16)
            for b in range(1, B):
                load_x(b)
            store_parts(0, range(C))
            for g in range(NG):
                load_stack(0, g, 0)
            store_parts(0, range(C, 2 * C))
            for g in range(NG):
                load_stack(0, g, 1)
            store_rows(0)
            for g in range(NG):
                load_rows(0, g)
            load_ctx(1)
            load_pos(1)
            load_max_rows(0)
            store_parts(1, range(C))
            for s in range(STEPS):
                b, g = divmod(s, NG)
                more = b + 1 < B
                if g == 0:
                    if more and b:
                        load_ctx(b + 1)
                    if b:
                        load_group(b, 3)
                if g == 1 and more:
                    if b:
                        store_parts(b + 1, range(C, 2 * C))
                    if b + 2 < B:
                        load_pos(b + 2)
                if g >= 2 and more:
                    load_group(b + 1, g - 1)
                if s + 1 < STEPS:
                    load_max_rows(s + 1)
                if g == 0 and more:
                    store_parts(b + 1, range(C) if b else range(C, 2 * C))
                if g == 1 and more:
                    store_rows(b + 1)
                    load_group(b + 1, 0)
                if s == STEPS - 3:
                    for e in range(NRAW):
                        load_expert(e)
                if g == 3 and b >= 2:
                    store_scores(b - 2)

            def load_scores(n):
                b, e = divmod(n, E)
                if n == 0:
                    sp.wait_ge(qk_done, EXPS)
                if e == 0:
                    sp.wait_ge(sc_out, 16 * (b + 1))
                if n >= 3:
                    sp.wait_ge(t1_done, n - 2)
                sp.dma_start(sbc[:, n % 3, :], sc_dram[e:e + 1, b * S:(b + 1) * S].broadcast_to([P, S])
                             ).then_inc(in_scores[n % 3], 16)

            def store_out(b):
                sp.wait_ge(osb_done, b + 1)
                sp.dma_start(out_t[:, b * S:(b + 1) * S].rearrange("(c p) s -> p c s", p=P),
                             osb[:, :, :]).then_inc(out_done, 16)

            for n in range(3):
                load_scores(n)
            for n in range(B * E):
                if n + NRAW < E:
                    load_expert(n + NRAW)
                if n + 3 < B * E:
                    load_scores(n + 3)
                if n == 10:
                    store_scores(B - 2)
                if n == 19:
                    store_scores(B - 1)
                if n % E == 8 and n >= E:
                    store_out(n // E - 1)
            store_out(B - 1)
            sp.wait_ge(out_done, 16 * B)

        @block.gpsimd
        def _(pool):
            links = [0]

            def link(ins):
                links[0] += 1
                ins.then_inc(pool_chain, 1)
                pool.wait_ge(pool_chain, links[0])

            pool.memset(nhalf[:, :], -0.5)
            link(pool.memset(ident[:, :], 0.0))
            link(pool.affine_select(out=ident[:, :], in_=ident[:, :], compare_op=ALU.not_equal, fill=1.0,
                                    base=0, pattern=[[-1, P]], channel_multiplier=1))
            pool.tensor_copy(ident_h[:, :], ident[:, :])
            pool.tensor_scalar(ident_w[:, :], ident[:, :], WS, None, ALU.mult).then_inc(idents, 1)
            pool.memset(pe[:, :, E:E + TOPK], -1.0)
            pool.memset(nf[:, NT:], 0.0)
            pool.memset(brow, 0.0).then_inc(brow_zero, 1)
            link(pool.memset(ones[:, :], 1.0))
            pool.affine_select(out=before[:, :], in_=ones[:, :], compare_op=ALU.is_gt, fill=0.0,
                               base=0, pattern=[[1, P]], channel_multiplier=-1)
            pool.memset(V[:, :, HD:2 * HD], 1.0).then_inc(ones_set, 1)

            def norm_rstd(what, b):
                n = NORM[what, b]
                pool.wait_ge(veps_done, n + 1)
                if what == "y" and b + 2 < B:
                    pool.wait_ge(w_full, RING["xT", b + 2] + 1)
                elif what == "y":
                    pool.wait_ge(w_full, RING["nT", b - 1] + 1)
                elif b >= 3:
                    pool.wait_ge(w_full, RING["nT", b - 3] + 1)
                elif b:
                    pool.wait_ge(w_full, RING["xT", b - 1] + 1)
                link(pool.tensor_tensor(rstd[:, :], veps[:, :], nhalf[:, :], ALU.pow))
                if what == "y":
                    link(pool.tensor_scalar(rstd[:, :], rstd[:, :], XS, None, ALU.mult))

            def norm_tile(b, t):
                return pool.tensor_scalar(xn[:, t, :], x_sb[:, b * NT + t, :], mv[:, t, 0:1], rstd[:, t:t + 1],
                                          ALU.subtract, ALU.mult)

            def normalise(what, b):
                norm_rstd(what, b)
                for t in range(NT):
                    ins = norm_tile(b, t)
                ins.then_inc(norm_done, 1)
                pool.wait_ge(norm_done, NORM[what, b] + 1)

            def split_into(out, v):
                for i in range(PARTS - 1):
                    link(pool.tensor_scalar(out[:, i, :], v, 1.0, 1.0, ALU.mult, ALU.mult))
                    last = i == PARTS - 2
                    ins = pool.tensor_tensor(out[:, i + 1, :] if last else v, v, out[:, i, :], ALU.subtract)
                    if not last:
                        link(ins)
                return ins

            def split(n):
                pool.wait_ge(qk_full, n + 1)
                if n >= 2:
                    pool.wait_ge(parts_out[n % 2], 16 * (n // 2))
                ins = split_into(parts[:, n % 2, :, :], qk32[:, n % 2, :])
                ins.then_inc(parts_done, 1)

            def distances(b, tiles):
                if b >= 2:
                    pool.wait_ge(step_done, (b - 1) * NG)
                for r in tiles:
                    n = b * NT + r
                    pool.wait_ge(sq_done, n + 1)
                    o = d2[:, b % 2, r, :]
                    link(pool.tensor_tensor(o, sq[:, n % 2, 0, :], sq[:, n % 2, 1, :], ALU.add))
                    pool.tensor_tensor(o, sq[:, n % 2, 2, :], o, ALU.subtract).then_inc(d2_sum, 1)
                    pool.wait_ge(d2_sum, n + 1)
                    own = o[:, r * P:(r + 1) * P]
                    pool.affine_select(out=own, in_=own, compare_op=ALU.not_equal, fill=-FAR, base=0,
                                       pattern=[[-1, P]], channel_multiplier=1).then_inc(d2_done, 1)

            def split_rows(b):
                pool.wait_ge(brow_done, b + 1)
                if b:
                    pool.wait_ge(rows_out, 32 * b)
                split_into(nparts, brow).then_inc(rows_done, 1)

            def reduce_extremes(b):
                pool.wait_ge(ext_done, b + 1)
                pool.partition_all_reduce(extr[:, :], ext[:, :], P, RMAX).then_inc(extr_done, 1)

            def residual(b):
                if b == 0:
                    pool.wait_ge(tabs_done, 1)
                xs = x_sb[:, b * NT:(b + 1) * NT, :]
                pool.tensor_tensor(xs, xs, bo_sb[:, None, :].broadcast_to([P, NT, D]), ALU.add).then_inc(xb_done, 1)

            norm_rstd("x", 0)
            pool.sem_inc(rstd_done, 1)
            distances(0, range(NT))
            reduce_extremes(0)
            split_rows(0)
            residual(0)
            normalise("x", 1)
            for n in range(2 * C, 3 * C):
                split(n)
            for s in range(STEPS):
                b, g = divmod(s, NG)
                if b + 1 < B:
                    if g == 0:
                        distances(b + 1, range(0, 2))
                    ns = range(2 * C * (b + 1) + C * g, 2 * C * (b + 1) + C * (g + 1)) if g < 2 else ()
                    if b == 0:
                        ns = range(3 * C, 4 * C) if g == 0 else ()
                    for n in ns[:1]:
                        split(n)
                    if g == 1:
                        reduce_extremes(b + 1)
                    for n in ns[1:]:
                        split(n)
                    if g == 0:
                        distances(b + 1, range(2, NT))
                    if g == 1:
                        split_rows(b + 1)
                if g == 2 and b >= 1:
                    normalise("y", b - 1)
                if g == 2 and b + 1 < B:
                    residual(b + 1)
                if g == 3 and b + 2 < B:
                    normalise("x", b + 2)
            for n in range(B * E):
                if n == 4:
                    norm_rstd("y", B - 1)
                if 5 <= n < 5 + NT:
                    ins = norm_tile(B - 1, n - 5)
                    if n == 4 + NT:
                        ins.then_inc(norm_done, 1)
                pool.wait_ge(silu_done, n + 1)
                pool.wait_ge(in_scores[n % 3], 16 * (n // 3 + 1))
                if n >= 2:
                    pool.wait_ge(act_done, n - 1)
                pool.tensor_tensor(t1[:, n % 2, :], sg[:, n % 2, :], sbc[:, n % 3, :], ALU.mult).then_inc(t1_done, 1)

        @block.scalar
        def _(act):
            act.dma_start(npos[:, :, :], pos_cols).then_inc(in_small, 16)
            act.dma_start(pos_sb[:, :], pos[0:1, :].broadcast_to([P, S * 3])).then_inc(in_pos, 16)
            act.dma_start(bqk[:, :, :], bqk_cols).then_inc(in_bqk, 16)
            act.wait_ge(in_small, 16)
            nc.scalar.mul(npos[:, :, :], npos[:, :, :], -1.0).then_inc(npos_done, 1)
            act.wait_ge(npos_done, 1)

            def square(n, a):
                if a == 0:
                    act.wait_ge(in_pos, 16 * (n // NT + 1))
                    if n >= 2:
                        act.wait_ge(d2_sum, n - 1)
                v = pos_sb[:, :].rearrange("p (s a) -> p a s", a=3)
                if a < 3:
                    ins = nc.scalar.activation(sq[:, n % 2, a, :], v[:, a, :], ACT.Square, bias=npos[:, n, a:a + 1])
                    if a == 2:
                        ins.then_inc(sq_neg, 1)
                else:
                    act.wait_ge(sq_neg, n + 1)
                    nc.scalar.mul(sq[:, n % 2, 2, :], sq[:, n % 2, 2, :], -1.0).then_inc(sq_done, 1)

            def router_exp(b):
                act.wait_ge(lg_done, b + 1)
                nc.scalar.activation(pe[:, :, 0:E], lg[:, :, :], ACT.Exp, scale=1.0 / (XS * WS)).then_inc(lgexp_done, 1)

            def projected(kind, b):
                w = RING[kind, b]
                act.wait_ge(w_full, w + 1)
                t = W[w % 2]
                if kind == "xT":
                    nc.scalar.copy(xnT[:, :, :].rearrange("p c s -> p (c s)"), t[:, :]).then_inc(w_free[w % 2], 1)
                elif kind == "nT":
                    nc.scalar.copy(x2T[:, 0, :, b * S:(b + 1) * S],
                                   t[:, :].rearrange("p (c s) -> p c s", c=C)).then_inc(x2h_done, 1)
                else:
                    i = "kq".index(kind)
                    if b == 0 and i == 0:
                        act.wait_ge(in_bqk, 16)
                        nc.scalar.mul(bqk[:, 1, :], bqk[:, 1, :], QSCALE).then_inc(bq_scaled, 1)
                        act.wait_ge(bq_scaled, 1)
                    for c in range(C):
                        n = 2 * C * b + C * i + c
                        if n >= 2:
                            act.wait_ge(parts_done, n - 1)
                        nc.scalar.activation(qk32[:, n % 2, :], t[:, c * S:(c + 1) * S], ACT.Identity,
                                             bias=bqk[:, i, c:c + 1], scale=(1.0, QSCALE)[i]).then_inc(qk_full, 1)
                    act.wait_ge(qk_full, 2 * C * b + C * (i + 1))
                    act.sem_inc(w_free[w % 2], 1)

            def split_high_w13(e):
                act.wait_ge(in_raw[e % NRAW], 48 * (e // NRAW + 1))
                if e == 8:
                    act.wait_ge(step_done, STEPS)
                nc.scalar.activation(w13(e)[:, 0, :, :], raw[:, e % NRAW, 0:2 * D].rearrange("p (m i) -> p m i", i=P),
                                     ACT.Copy, scale=WS).then_inc(w13_high, 1)

            def split_high_w2(e):
                if e == 0:
                    act.wait_ge(pv_done, STEPS * NT)
                nc.scalar.activation(w2s[:, e, 0, :], raw[:, e % NRAW, 2 * D:3 * D], ACT.Copy, scale=WS).then_inc(w2_high, 1)

            for kind, tile in (("", 0), ("", 1), ("k", None), ("xT", 2), ("", 3), ("q", None)):
                if kind == "k":
                    act.wait_ge(in_gates, 32)
                    nc.scalar.activation(tg[:, :], tg[:, :], ACT.Tanh).then_inc(tg_done, 1)
                if kind:
                    projected(kind, 0)
                if tile is not None:
                    for a in range(4):
                        square(tile, a)
            for kind, tile in (("k", NT), ("xT", NT + 1), ("q", None)):
                projected(kind, 1)
                if tile is not None:
                    for a in range(4):
                        square(tile, a)
            for s in range(STEPS):
                b, g = divmod(s, NG)
                for unit, e in step_units(s, 0) + step_units(s, 1):
                    if unit == "x":
                        for kind, xb in extras(s, e):
                            if kind in BY_ACT or kind == "nT":
                                projected(kind, xb)
                    if unit != "e":
                        continue
                    n = s * NE + e
                    act.wait_ge(qk_done, n + 1)
                    act.wait_ge(granted, n + 1)
                    if n >= NP_RING:
                        act.wait_ge(pv_done, (n - NP_RING) // G + 1)
                    nc.scalar.activation(pr[:, n % NP_RING, :], SC[n % 3][:, :], ACT.Exp).then_inc(exp_done, 1)
                    if s >= STEPS - 2 and e in (4, 9):
                        split_high_w13(2 * (s - STEPS + 2) + e // 5)
                    if e % 2 == 0 and g == 3 and b + 2 < B:
                        square((b + 2) * NT + e // 8, e // 2 % 4)
                    if e % 2 == 0 and g == 0 and b + 1 < B:
                        square((b + 1) * NT + 2 + e // 8, e // 2 % 4)
                    if g == 2 and b >= 2 and e == 1:
                        router_exp(b - 2)

            router_exp(B - 2)
            for n in range(B * E):
                for kind, b in LATE.get(n - 1, []):
                    if kind == "nT":
                        projected(kind, b)
                w = RING["gu", n]
                act.wait_ge(w_full, w + 1)
                if n >= 2:
                    act.wait_ge(t1_done, n - 1)
                nc.scalar.activation(sg[:, n % 2, :], W[w % 2][:, 0:S], ACT.Silu, scale=1.0 / (XS * WS)).then_inc(silu_done, 1)
                for e in (0, 1, 2) if n == 0 else (n + 2,) if n + 2 < E else ():
                    split_high_w2(e)
                if NRAW <= n + 3 < E:
                    split_high_w13(n + 3)
                if n == 14:
                    router_exp(B - 1)

        @block.vector
        def _(dve):
            links, w, norms = [0], [0], [0]

            def link(ins):
                links[0] += 1
                ins.then_inc(dve_chain, 1)
                dve.wait_ge(dve_chain, links[0])

            def slot():
                dve.wait_ge(w_full, w[0] + 1)
                return W[w[0] % 2]

            def used(ins):
                ins.then_inc(w_free[w[0] % 2], 1)
                w[0] += 1

            def norm_stats(b):
                if norms[0]:
                    dve.wait_ge(norm_done, norms[0])
                norms[0] += 1
                for t in range(NT):
                    ins = dve.bn_stats(st[:, t, :], x_sb[:, b * NT + t, :])
                link(ins)
                for t in range(NT):
                    ins = dve.bn_aggr(mv[:, t, :], st[:, t, :])
                link(ins)
                dve.tensor_scalar(veps[:, :], mv[:, :, 1], EPS, None, ALU.add).then_inc(veps_done, 1)

            def extremes(b, tiles):
                for r in tiles:
                    dve.wait_ge(d2_done, NT * b + r + 1)
                    ins = dve.max(m8[:, r, :], d2[:, b % 2, r, :])
                if NT - 1 not in tiles:
                    return
                if b:
                    dve.wait_ge(extr_done, b)
                link(ins)
                dve.tensor_scalar(nf[:, 0:NT], m8[:, :, 0], -NEAR, None, ALU.is_gt).then_inc(nf_done, 1)
                dve.tensor_reduce(ext[:, 0:1], m8[:, :, 0], AX.X, ALU.max)
                link(dve.scalar_tensor_tensor(out=near8[:, :, :], in0=m8[:, :, :], scalar=-NEAR, in1=m8[:, :, :],
                                              op0=ALU.is_gt, op1=ALU.mult))
                dve.tensor_reduce(ext[:, 1:2], near8[:, :, :], AX.XY, ALU.min, negate=True).then_inc(ext_done, 1)

            many = {}

            def choose_slots(b, t):
                link(dve.tensor_scalar(few[:, 0:1], t[:, NT:NT + 1], NSLOT + 0.5, None, ALU.is_lt))
                link(dve.tensor_scalar(few[:, 1:2], few[:, 0:1], 1.0, None, ALU.is_lt))
                dve.tensor_copy(flags[:, b, 0:1], few[:, 1:2])
                link(dve.tensor_scalar(nslot[:, :], nf[:, 0:NT], few[:, 0:1], None, ALU.mult))
                link(dve.scalar_tensor_tensor(out=nslot[:, :], in0=t[:, 0:NT], scalar=1.0, in1=nslot[:, :],
                                              op0=ALU.add, op1=ALU.mult))
                dve.tensor_tensor(sel.rearrange("p (t n) -> p t n", t=NT), nslot[:, :, None].broadcast_to([P, NT, P]),
                                  slot_of[:, None, :].broadcast_to([P, NT, P]), ALU.is_equal).then_inc(sel_done, 1)

            def near_rows(b, t):
                if b:
                    dve.wait_ge(rows_out, 32 * b)
                else:
                    dve.wait_ge(brow_zero, 1)
                dve.tensor_copy(selT, t[:, S:2 * S])
                many[b], any_ = (dve.value_load(flags[0:1, b, i:i + 1], min_val=0, max_val=1) for i in range(2))
                with dve.If(any_ > 0):
                    lo, hi = (dve.value_load(flags[0:1, b, i:i + 1], min_val=0, max_val=BINS) for i in (2, 3))
                    dist = t[:, 0:S]
                    dve.tensor_scalar(brow, dist, -NEAR, drow[:, bass.ds(hi, 1)], ALU.is_gt, ALU.mult)
                    dve.drain()
                    with dve.If(hi > lo):
                        with dve.Fori(lo + 1, hi + 1) as j:
                            dve.tensor_scalar(btmp, dist, nthr_sb[:, bass.ds(j, 1)], grow[:, bass.ds(j, 1)],
                                              ALU.is_gt, ALU.mult)
                            dve.drain()
                            dve.tensor_tensor(brow, brow, btmp, ALU.add)
                            dve.drain()
                dve.drain().then_inc(brow_done, 1)

            def near_flags(b):
                dve.wait_ge(extr_done, b + 1)
                dve.tensor_scalar(flags_f[:, 1:2], extr[:, 0:1], -NEAR, None, ALU.is_gt)
                link(dve.tensor_scalar(extr[:, 1:2], extr[:, 1:2], -1.0, None, ALU.mult))
                for i in range(2):
                    link(dve.tensor_scalar(cmp_[:, :], nthr_sb[:, 1:BINS + 1], extr[:, i:i + 1], None, ALU.is_ge))
                    link(dve.tensor_reduce(flags_f[:, 2 + i:3 + i], cmp_[:, :], AX.X, ALU.add))
                link(dve.tensor_copy(flags[:, b, 1:4], flags_f[:, 1:4]))

            def split_parts(out, v):
                for i in range(PARTS):
                    dve.tensor_copy(out[:, i, :], v)
                    dve.drain()
                    if i + 1 < PARTS:
                        dve.tensor_tensor(v, v, out[:, i, :], ALU.subtract)
                        dve.drain()

            def correct(tile, b, r, h):
                dist = d2[:, b % 2, r, :]
                with dve.Fori(1, BINS + 1) as j:
                    dve.tensor_scalar(btmp, dist, nthr_sb[:, bass.ds(j, 1)], gtab[:, bass.ds(j * H + h, 1)],
                                      ALU.is_gt, ALU.mult)
                    dve.drain()
                    dve.tensor_tensor(tile, tile, btmp, ALU.add)
                    dve.drain()

            def row_max(s, qt, pair, tile):
                h = G * (s % NG) + 2 * pair
                return dve.tensor_reduce(mneg[:, h:h + 2, qt], tile[:, :].rearrange("p (h k) -> p h k", h=2), AX.X, ALU.max, negate=True)

            def exp_tile(s, e):
                b, g = divmod(s, NG)
                n = s * NE + e
                dve.wait_ge(qk_done, n + 1)
                correct(SC[n % 3][:, :], b, e // G, e % G + G * g)
                dve.drain().then_inc(granted, 1)

            def max_slot(s, m, near):
                b, g = divmod(s, NG)
                t = slot()
                if near:
                    with dve.If(many[b] > 0):
                        for h in range(2):
                            correct(t[:, h * S:(h + 1) * S], b, m // 2, G * g + 2 * (m % 2) + h)
                used(row_max(s, m // 2, m % 2, t))

            def grant(s):
                with dve.If(many[s // NG] < 1):
                    dve.sem_inc(granted, NE)

            def tiles(s, half, near):
                if half and s + 1 < STEPS:
                    dve.drain().then_inc(m_done, 1)
                for kind, i in step_units(s, half):
                    if kind == "x":
                        if s >= 0 or i > 0:
                            for what, b in extras(s, i):
                                if what != "nr":
                                    extra(what, b)
                        between(s, i)
                    if kind == "m":
                        max_slot(*i, near)
                    if kind == "t":
                        max_parts(i)
                    if kind == "e" and near:
                        with dve.If(many[s // NG] > 0):
                            exp_tile(s, i)

            def units(s, halves):
                b, nb = max(s, 0) // NG, min(s + 1 + halves[-1], STEPS - 1) // NG
                start = w[0], links[0], norms[0]
                with dve.If(many[b] + many[nb] > 0):
                    for half in halves:
                        tiles(s, half, True)
                after = w[0], links[0], norms[0]
                w[0], links[0], norms[0] = start
                with dve.Else():
                    for half in halves:
                        tiles(s, half, False)
                assert after == (w[0], links[0], norms[0])

            def step(s):
                if ("nr", s // NG + 1) in extras(s, NM // 2):
                    units(s, (0,))
                    extra("nr", s // NG + 1)
                    units(s, (1,))
                else:
                    units(s, (0, 1))
                if 0 <= s < STEPS - 1:
                    grant(s + 1)
                dve.drain().then_inc(step_done, 1)

            def split_low_w13(e):
                dve.wait_ge(w13_high, e + 1)
                dve.scalar_tensor_tensor(out=w13(e)[:, 1, :, :].rearrange("p m i -> p (m i)"), in0=raw[:, e % NRAW, 0:2 * D],
                                         scalar=WS, in1=w13(e)[:, 0, :, :].rearrange("p m i -> p (m i)"),
                                         op0=ALU.mult, op1=ALU.subtract).then_inc(w13_low, 1)

            def split_low_w2(e):
                dve.wait_ge(w2_high, e + 1)
                dve.scalar_tensor_tensor(out=w2s[:, e, 1, :], in0=raw[:, e % NRAW, 2 * D:3 * D], scalar=WS,
                                         in1=w2s[:, e, 0, :], op0=ALU.mult, op1=ALU.subtract).then_inc(w2_low, 1)

            def between(s, place):
                b, g = divmod(s, NG)
                if s < 0:
                    return
                if g == 3 and place == 4 and b + 2 < B:
                    dve.wait_ge(in_x[b + 2], 16)
                    norm_stats(b + 2)
                if g == 2 and place == 3 and b:
                    dve.wait_ge(*freed(RING["wo", b - 1]))
                    norm_stats(b - 1)
                if g == 3 and place == 2 and b >= 2:
                    router(b - 2)
                if s >= STEPS - 2 and place in (3, 6):
                    split_low_w13(2 * (s - STEPS + 2) + place // 3 - 1)
                if place == 1 and s >= 1:
                    norm_out(s - 1)
                if g == 1 and b + 1 < B and place in (1, 2):
                    extremes(b + 1, (2 * place - 2, 2 * place - 1))

            def max_parts(s):
                g = s % NG
                t = slot()[0:H, 0:P]
                link(dve.tensor_copy(mpart[:, g, 0, :], t))
                for i in range(1, PARTS):
                    link(dve.tensor_tensor(mtmp[:, :], t if i == 1 else mtmp[:, :], mpart[:, g, i - 1, :], ALU.subtract))
                    if i + 1 < PARTS:
                        link(dve.tensor_copy(mpart[:, g, i, :], mtmp[:, :]))
                dve.tensor_copy(mpart[:, g, PARTS - 1, :], mtmp[:, :]).then_inc(m_split, 1)
                used(dve.drain())

            def norm_out(s):
                pair, odd = divmod(s, 2)
                dve.wait_ge(pv_done, NT * (s + 1))
                q3, p3 = (v[:, :].rearrange("p (q d) -> p q d", d=32) for v in (rec, opair))
                dve.transpose(rec[:, :], O[:, :]).then_inc(o_read, 1)
                dve.wait_ge(o_read, s + 1)
                link(dve.reciprocal(rs[:, :], q3[:, :, HD]))
                if s >= 2 and not odd:
                    dve.wait_ge(oT_done, pair)
                link(dve.tensor_tensor(p3[:, :, odd * HD:(odd + 1) * HD], q3[:, :, 0:HD],
                                       rs[:, :, None].broadcast_to([P, S // 32, HD]), ALU.mult))
                if odd:
                    if s % NG == 1 and s > NG:
                        dve.wait_ge(w_full, RING["wo", s // NG - 1] + 1)
                    dve.transpose(oT[:, pair % 2, :], opair[:, :]).then_inc(oT_done, 1)

            def router(b):
                def per_token(v):
                    return v[:, :, None].broadcast_to([P, NT, E])

                dve.wait_ge(lgexp_done, b + 1)
                p_ = pe[:, :, 0:E]
                link(dve.tensor_reduce(r4[:, :], p_, AX.X, ALU.add))
                link(dve.reciprocal(r4[:, :], r4[:, :]))
                link(dve.tensor_tensor(p_, p_, per_token(r4), ALU.mult))
                for t in range(NT):
                    ins = dve.max(top[:, t, :], pe[:, t, 0:E])
                link(ins)
                link(dve.memset(top[:, :, TOPK:8], -1.0))
                for t in range(NT):
                    ins = dve.match_replace(mr[:, t, :], top[:, t, :], pe[:, t, :], -2.0)
                link(ins)
                link(dve.scalar_tensor_tensor(out=score[:, :, :], in0=mr[:, :, 0:E], scalar=-1.5, in1=p_,
                                              op0=ALU.is_lt, op1=ALU.mult))
                link(dve.tensor_reduce(r4[:, :], score[:, :, :], AX.X, ALU.add))
                link(dve.reciprocal(r4[:, :], r4[:, :]))
                link(dve.tensor_scalar(r4[:, :], r4[:, :], tg[:, 1:2], None, ALU.mult))
                dve.tensor_tensor(score[:, :, :], score[:, :, :], per_token(r4), ALU.mult).then_inc(score_done, 1)

            def extra(kind, b):
                if kind in BY_ACT:
                    w[0] += 1
                    return
                if kind == "sc" and b:
                    dve.wait_ge(sc_out, 16 * b)
                if kind == "nr":
                    near_flags(b)
                t = slot()
                if kind == "rk":
                    choose_slots(b, t)
                    used(dve.drain())
                elif kind == "nr":
                    near_rows(b, t)
                    used(dve.drain())
                elif kind == "v":
                    dve.wait_ge(pv_done, NT * NG * b) if b else dve.wait_ge(ones_set, 1)
                    used(dve.tensor_tensor(V[:, :, 0:HD].rearrange("p (t h) d -> p t h d", t=NT),
                                           t[:, :].rearrange("p (t h d) -> p t h d", t=NT, h=H),
                                           bv_sb[:, :].rearrange("p (o h d) -> p o h d", o=1, h=H).broadcast_to([P, NT, H, HD]),
                                           ALU.add))
                elif kind == "wo":
                    dve.wait_ge(xb_done, b + 1)
                    xs = x_sb[:, b * NT:(b + 1) * NT, :].rearrange("p t d -> p (t d)")
                    used(dve.scalar_tensor_tensor(out=xs, in0=t[:, :], scalar=tg[:, 0:1], in1=xs,
                                                  op0=ALU.mult, op1=ALU.add))
                elif kind == "nT":
                    cols = slice(b * S, (b + 1) * S)
                    t3 = t[:, :].rearrange("p (c s) -> p c s", c=C)
                    dve.wait_ge(x2h_done, b + 1)
                    used(dve.tensor_tensor(x2T[:, 1, :, cols], t3, x2T[:, 0, :, cols], ALU.subtract))
                elif kind == "lg":
                    t3 = t[:, 0:NT * E].rearrange("p (t e) -> p t e", t=NT)
                    link(dve.tensor_reduce(r4[:, :], t3, AX.X, ALU.max))
                    dve.tensor_tensor(lg[:, :, :], t3, r4[:, :, None].broadcast_to([P, NT, E]),
                                      ALU.subtract).then_inc(lg_done, 1)
                    used(dve.drain())
                elif kind == "sc":
                    dve.tensor_copy(scT[:, :], t[0:E, 0:S]).then_inc(scT_done, 1)
                    used(dve.drain())

            dve.memset(Kst[ROWS:P, :, :].rearrange("p h s -> p (h s)").bitcast(F32), TWO_ONES)
            dve.wait_ge(in_x[0], 16)
            norm_stats(0)
            dve.wait_ge(rstd_done, 1)
            for t in range(NT):
                ins = dve.tensor_scalar(xn[:, t, :], x_sb[:, t, :], mv[:, t, 0:1], rstd[:, t:t + 1],
                                        ALU.subtract, ALU.mult)
            ins.then_inc(norm_done, 1)
            dve.wait_ge(in_tab, 16 * 6)
            dve.wait_ge(tg_done, 1)
            dve.wait_ge(idents, 1)
            dve.memset(top[:, :, :], -1.0)
            link(dve.tensor_tensor(dtab[:, :].rearrange("p (j h) -> p j h", h=H), etab[:, :, :],
                                   etab[:, BINS:BINS + 1, :].broadcast_to([P, BINS + 1, H]), ALU.subtract))
            dve.tensor_tensor(gtab[:, H:], etab[:, 0:BINS, :].rearrange("p j h -> p (j h)"),
                              etab[:, 1:BINS + 1, :].rearrange("p j h -> p (j h)"), ALU.subtract)
            dve.tensor_scalar(drow[:, :], erow[:, :], erow[:, BINS:BINS + 1], None, ALU.subtract)
            dve.tensor_tensor(grow[:, 1:], erow[:, 0:BINS], erow[:, 1:BINS + 1], ALU.subtract)
            dve.tensor_scalar(bo_sb[:, :], bo_sb[:, :], tg[:, 0:1], None, ALU.mult).then_inc(tabs_done, 1)

            def split_first(n):
                dve.wait_ge(qk_full, n + 1)
                if n >= 2:
                    dve.wait_ge(parts_out[n % 2], 16 * (n // 2))
                split_parts(parts[:, n % 2, :, :], qk32[:, n % 2, :])
                dve.drain().then_inc(parts_done, 1)

            for kind, b in extras(-1, 0):
                if kind == "rk":
                    split_first(0)
                    split_first(1)
                    extremes(0, range(NT))
                    split_first(2)
                if kind == "v":
                    dve.wait_ge(in_vow, 16 * 3)
                if kind == "nr":
                    split_first(3)
                    for h in range(H):
                        ins = dve.tensor_scalar(diag[:, 0, h, :], ident[:, :], dtab[:, h:h + 1], None, ALU.mult)
                    ins.then_inc(tabs_done, 1)
                extra(kind, b)
            for h in range(H):
                dve.scalar_tensor_tensor(out=diag[:, 1, h, :], in0=ident[:, :], scalar=dtab[:, h:h + 1],
                                         in1=diag[:, 0, h, :], op0=ALU.mult, op1=ALU.subtract)
            link(dve.tensor_scalar(gate_h[:, 0, :, :], gate_sb[:, :, :], WS, None, ALU.mult))
            dve.scalar_tensor_tensor(out=gate_h[:, 1, :, :], in0=gate_sb[:, :, :], scalar=WS, in1=gate_h[:, 0, :, :],
                                     op0=ALU.mult, op1=ALU.subtract).then_inc(tabs_done, 1)
            grant(0)
            dve.wait_ge(in_x[1], 16)
            norm_stats(1)
            step(-1)
            for s in range(STEPS):
                step(s)

            def result(b):
                dve.wait_ge(w2_used, E * (b + 1))
                if b:
                    dve.wait_ge(out_done, 16 * b)
                for c in range(C):
                    ins = dve.tensor_scalar(osb[:, c, :], Y[b % 2][c][:, :], 1.0 / WS, None, ALU.mult)
                ins.then_inc(osb_done, 1)

            norm_out(STEPS - 1)
            for n in range(B * E):
                t = slot()
                dve.wait_ge(t1_done, n + 1)
                used(dve.scalar_tensor_tensor(out=ac[:, n % 2, :], in0=t[:, S:2 * S], scalar=1.0 / (XS * WS),
                                              in1=t1[:, n % 2, :], op0=ALU.mult, op1=ALU.mult))
                dve.wait_ge(*freed(w[0] - 1))
                if n >= 3:
                    dve.wait_ge(w2_used, n - 2)
                link(dve.tensor_copy(ahl[:, n % 3, 0, :], ac[:, n % 2, :]))
                dve.tensor_tensor(ahl[:, n % 3, 1, :], ac[:, n % 2, :], ahl[:, n % 3, 0, :], ALU.subtract).then_inc(act_done, 1)
                for e in (0, 1, 2) if n == 0 else (n + 2,) if n + 2 < E else ():
                    split_low_w2(e)
                if NRAW <= n + 3 < E:
                    split_low_w13(n + 3)
                for kind, b in LATE.get(n, []):
                    extra(kind, b)
                if n == 3:
                    dve.wait_ge(*freed(RING["wo", B - 1]))
                    norm_stats(B - 1)
                if n in (5, 15):
                    router(B - 2 if n == 5 else B - 1)
                if n % E == 2 and n >= E:
                    result(n // E - 1)
            result(B - 1)

        @block.tensor
        def _(pe_):
            mm, w, o_n = nc.tensor.matmul, [0], [0]

            def slot():
                if w[0] >= 2:
                    pe_.wait_ge(*freed(w[0] - 2))
                return W[w[0] % 2]

            def full(ins):
                w[0] += 1
                ins.then_inc(w_full, 1)

            def transposes(t):
                for c in range(C):
                    for k in range(NT):
                        ins = nc.tensor.transpose(t[:, c * S + k * P:c * S + (k + 1) * P], xn[:, k, c * P:(c + 1) * P],
                                                  ident[:, :])
                full(ins)

            def extra(kind, b):
                if kind == "xT":
                    pe_.wait_ge(norm_done, NORM["x", b] + 1)
                elif kind == "q":
                    pe_.wait_ge(*freed(RING["xT", b]))
                    if b == 0:
                        pe_.wait_ge(in_wq, 16)
                elif kind == "k":
                    pe_.wait_ge(in_ctx, 16 * (b + 1))
                    if b == 0:
                        pe_.wait_ge(in_wk, 16)
                elif kind == "v" and b == 0:
                    pe_.wait_ge(in_vow, 16 * 3)
                elif kind == "wo":
                    pe_.wait_ge(oT_done, 2 * (b + 1))
                elif kind == "nT":
                    pe_.wait_ge(norm_done, NORM["y", b] + 1)
                elif kind == "lg":
                    pe_.wait_ge(*freed(RING["nT", b]))
                elif kind == "sc":
                    pe_.wait_ge(score_done, b + 1)
                elif kind == "rk":
                    pe_.wait_ge(nf_done, b + 1)
                elif kind == "nr":
                    pe_.wait_ge(sel_done, b + 1)
                t = slot()
                if kind == "rk":
                    mm(t[:, 0:NT + 1], before[:, :], nf[:, :], start=True, stop=False, skip_group_check=True)
                    for i in range(1, NT + 1):
                        ins = mm(t[:, i:NT + 1], ones[:, :], nf[:, 0:NT + 1 - i], start=False, stop=(i == NT),
                                 skip_group_check=True)
                    full(ins)
                elif kind == "nr":
                    for k in range(NT):
                        mm(t[:, 0:S], sel[:, k * P:(k + 1) * P], d2[:, b % 2, k, :], start=(k == 0), stop=(k == NT - 1))
                    for k in range(NT):
                        ins = nc.tensor.transpose(t[:, S + k * P:S + (k + 1) * P], sel[:, k * P:(k + 1) * P],
                                                  ident[:, :])
                    full(ins)
                elif kind == "xT" or kind == "nT":
                    transposes(t)
                elif kind == "q" or kind == "k":
                    wt, src = (wq_sb, xnT) if kind == "q" else (wk_sb, cT)
                    for c in range(C):
                        for k in range(C):
                            ins = mm(t[:, c * S:(c + 1) * S], wt[:, k, c * P:(c + 1) * P], src[:, k, :],
                                     start=(k == 0), stop=(k == C - 1))
                    full(ins)
                elif kind == "v":
                    for k in range(NT):
                        for c in range(C):
                            ins = mm(t[:, k * D:(k + 1) * D], cT[:, c, k * P:(k + 1) * P], wv_sb[:, c, :],
                                     start=(c == 0), stop=(c == C - 1))
                    full(ins)
                elif kind == "wo":
                    for k in range(NT):
                        for g in range(NG // 2):
                            ins = mm(t[:, k * D:(k + 1) * D], oT[:, g, k * P:(k + 1) * P], wo_sb[:, g, :],
                                     start=(g == 0), stop=(g == NG // 2 - 1))
                    full(ins)
                elif kind == "lg":
                    pairs = [(c, i, j) for c in range(C) for i, j in ((0, 0), (0, 1), (1, 0))]
                    for k in range(NT):
                        for m, (c, i, j) in enumerate(pairs):
                            ins = mm(t[:, k * E:(k + 1) * E], x2T[:, i, c, b * S + k * P:b * S + (k + 1) * P],
                                     gate_h[:, j, c, :], start=(m == 0), stop=(m == len(pairs) - 1))
                    full(ins)
                elif kind == "sc":
                    for k in range(NT):
                        ins = nc.tensor.transpose(t[0:E, k * P:(k + 1) * P], score[:, k, :], ident[:, :])
                    full(ins)

            def exp_scores(s, e):
                b, g = divmod(s, NG)
                n, r, h = s * NE + e, e // G, G * g + e % G
                if n == 0:
                    pe_.wait_ge(tabs_done, 3)
                if e == 0:
                    pe_.wait_ge(m_in, 16 * PARTS * (s + 1))
                if n >= 3:
                    pe_.wait_ge(exp_done, n - 2)
                mm(SC[n % 3][:, :], Kst[0:KROWS, h, r * P:(r + 1) * P], Qst[0:KROWS, h, :], start=True, stop=False,
                   skip_group_check=True)
                for i in range(2):
                    ins = mm(SC[n % 3][:, r * P:(r + 1) * P], ident_h[:, :], diag[:, i, h, :], start=False,
                             stop=(i == 1), skip_group_check=True)
                ins.then_inc(qk_done, 1)

            def max_scores(s, m):
                b, g = divmod(s, NG)
                r = m // 2
                if m == 0:
                    pe_.wait_ge(stack_in[g], 16 * STACK_DMAS * (b + 1))
                t = slot()
                for i in range(2):
                    h = G * g + 2 * (m % 2) + i
                    mm(t[:, i * S:(i + 1) * S], Qst[0:NROWS, h, r * P:(r + 1) * P], Kst[0:NROWS, h, :],
                       start=True, stop=False, skip_group_check=True)
                    ins = mm(t[:, i * S + r * P:i * S + (r + 1) * P], ident_h[:, :], diag[:, 0, h, :],
                             start=False, stop=True, skip_group_check=True)
                full(ins)

            def max_transpose(s):
                pe_.wait_ge(m_done, s + 1)
                g = s % NG
                full(nc.tensor.transpose(slot()[0:H, 0:P], mneg[:, G * g:G * g + G, :].rearrange("p h t -> p (h t)"),
                                         ident[:, :]))

            def values(s, r):
                b, g = divmod(s, NG)
                if r == 0:
                    if s:
                        pe_.wait_ge(o_read, s)
                    if g == 0:
                        pe_.wait_ge(*freed(RING["v", b]))
                pe_.wait_ge(exp_done, s * NE + (r + 1) * G)
                for j in range(G):
                    n = s * NE + r * G + j
                    ins = mm(O[32 * j:32 * j + 32, :], V[:, r * H + G * g + j, :], pr[:, n % NP_RING, :],
                             start=(r == 0), stop=(r == NT - 1), skip_group_check=True)
                ins.then_inc(pv_done, 1)

            pe_.wait_ge(idents, 1)
            for s in range(-1, STEPS):
                late = s >= 1
                for kind, i in step_units(s, 0) + step_units(s, 1):
                    if kind == "x":
                        for what, b in extras(s, i):
                            extra(what, b)
                            if late:
                                values(s - 1, NT - 1)
                                late = False
                        if s == -1 and i == 0:
                            pe_.wait_ge(tabs_done, 2)
                            pe_.wait_ge(ones_set, 1)
                    if kind == "e":
                        exp_scores(s, i)
                        if i == 1 and late:
                            values(s - 1, NT - 1)
                            late = False
                        if i % G == 1 and i > G:
                            values(s, i // G - 1)
                    if kind == "m":
                        max_scores(*i)
                    if kind == "t":
                        max_transpose(i)

            def gate_up(n):
                b, e = divmod(n, E)
                if b == 0:
                    pe_.wait_ge(w13_low, e + 1)
                if e == 0:
                    pe_.wait_ge(*freed(RING["nT", b]))
                t = slot()
                for m in range(2):
                    pairs = [(c, i, j) for c in range(C) for i, j in ((0, 0), (0, 1), (1, 0))]
                    for k, (c, i, j) in enumerate(pairs):
                        ins = mm(t[:, m * S:(m + 1) * S], w13(e)[:, i, C * m + c, :], x2T[:, j, c, b * S:(b + 1) * S],
                                 start=(k == 0), stop=(k == len(pairs) - 1))
                full(ins)

            def down(n):
                b, e = divmod(n, E)
                pe_.wait_ge(act_done, n + 1)
                if b == 0:
                    pe_.wait_ge(w2_low, e + 1)
                if n == 0:
                    pe_.wait_ge(exp_done, EXPS)
                if n == E:
                    pe_.wait_ge(o_read, STEPS)
                if e == 0 and b >= 2:
                    pe_.wait_ge(osb_done, b - 1)
                y = Y[b % 2]
                for c in range(C):
                    for k, (i, j) in enumerate(((0, 0), (0, 1), (1, 0))):
                        ins = mm(y[c][:, :], w2s[:, e, i, c * P:(c + 1) * P], ahl[:, n % 3, j, :],
                                 start=(e == 0 and k == 0), stop=(e == E - 1 and k == 2), skip_group_check=True)
                ins.then_inc(w2_used, 1)
                if e == 0:
                    for c in range(C):
                        for k in range(NT):
                            mm(y[c][:, k * P:(k + 1) * P], x_sb[:, b * NT + k, c * P:(c + 1) * P], ident_w[:, :],
                               start=False, stop=False, skip_group_check=True)

            values(STEPS - 1, NT - 1)
            for n in range(B * E):
                gate_up(n)
                for kind, b in LATE.get(n, []):
                    extra(kind, b)
                if n >= 2:
                    down(n - 2)
            down(B * E - 2)
            down(B * E - 1)


def kernel(**inputs):
    import concourse.bacc as bacc
    from concourse.bass_utils import run_bass_kernel_spmd

    a = {k: np.asarray(v) for k, v in inputs.items()}

    def by_dim(v):
        return np.swapaxes(v.reshape(v.shape[:-1] + (C, H // C, HD)), -1, -2).reshape(v.shape)

    pos_ = a["fside_BxSx3_0"]
    given = {
        "x": a["x"],
        "ctx_t": a["ctx_1024"].reshape(B * S, D).T,
        "pos": pos_.reshape(B, S * 3),
        "pos_cols": pos_.reshape(B * NT, P, 3).transpose(1, 0, 2),
        "g_x": a["g_xattn"], "g_f": a["g_ffn"],
        "wq": by_dim(a["L0_xattn_Wq"]), "wk": by_dim(a["L0_xattn_Wk"]),
        "bqk_cols": np.stack([by_dim(a["L0_xattn_bk"]).reshape(C, P), by_dim(a["L0_xattn_bq"]).reshape(C, P)]).transpose(2, 0, 1),
        "wv": a["L0_xattn_Wv"], "bv": a["L0_xattn_bv"], "bo": a["L0_xattn_bo"],
        "wo": a["L0_xattn_Wo"].reshape(NG // 2, 2, G, HD, D).transpose(2, 1, 3, 0, 4).reshape(P, NG // 2, D),
        "emb": a["L0_xattn_dist_emb"], "emb_rows": np.tile(a["L0_xattn_dist_emb"].T, (NSLOT, 1)), "gate_t": a["L0_ffn_gate_w"].T,
        "w1": a["L0_ffn_w1"], "w3": a["L0_ffn_w3"], "w2": a["L0_ffn_w2"], "nthr": -THRESHOLDS,
        "slots": np.repeat(np.arange(1, NSLOT + 1, dtype=np.float32), H)[None, :],
    }
    nc = bacc.Bacc("TRN2", target_bir_lowering=False, num_devices=1)
    arrays, args = {}, {}
    for name, v in given.items():
        v = np.ascontiguousarray(v)
        arrays[f"in_{name}"] = v
        args[name] = nc.dram_tensor(f"in_{name}", v.shape, mybir.dt.from_np(v.dtype), kind="ExternalInput").ap()
    args["out_t"] = nc.dram_tensor("out_t", (D, B * S), F32, kind="ExternalOutput").ap()
    gated_block(nc, **args)
    got = run_bass_kernel_spmd(nc, [arrays], core_ids=[0]).results[0]["out_t"]
    return np.ascontiguousarray(got.T).reshape(B, S, D)
```
